# Optimizing a Trainium2 kernel written in Bass

```python
import numpy as np
import jax
import jax.numpy as jnp

def _softmax(x, axis=-1):
    return jax.nn.softmax(x, axis=axis)

def _gelu(x):
    return jax.nn.gelu(x, approximate=True)

def _silu(x):
    return jax.nn.silu(x)

def _sigmoid(x):
    return jax.nn.sigmoid(x)

def _layernorm(x, axis=-1, eps=1e-05):
    m = jnp.mean(x, axis=axis, keepdims=True)
    v = jnp.var(x, axis=axis, keepdims=True)
    return (x - m) / jnp.sqrt(v + eps)

def _scatter_add(tgt, idx, src, axis=0):
    return tgt.at[idx].add(src)

def _segment_sum(src, seg, n):
    return jax.ops.segment_sum(src, seg, n)
kernel_name = 'mk_conv_preact_d4_conv_nchw16_r4_758e38'

def setup_inputs(seed: int=0):
    np.random.seed(seed)
    _w = jnp.asarray

    def _rec_inputs():
        import jax
        import jax.numpy as jnp
        _gk = jax.random.key(seed)
        x = -7.109e-05 + 0.9999 * jax.random.normal(jax.random.fold_in(_gk, 1), (8, 16, 128, 128), jnp.float32)
        return x
    x = _rec_inputs()

    def _L0_conv_setup():
        import jax, jax.numpy as jnp
        import numpy as np
        B, CIN, COUT, H, W = (16, 16, 16, 128, 128)
        KH, KW = (3, 3)
        STRIDE = 1
        PAD = 1
        key = jax.random.key(seed)
        k1, k2, k3 = jax.random.split(key, 3)
        std_w = 6.0 / (CIN + COUT)
        x = jax.random.normal(k1, (B, CIN, H, W), dtype=jnp.float32)
        weights = jax.random.uniform(k2, (COUT, CIN, KH, KW), dtype=jnp.float32, minval=-std_w, maxval=std_w)
        biases = jax.random.uniform(k3, (COUT,), dtype=jnp.float32, minval=-std_w, maxval=std_w)
        return {'x': x, 'weights': weights, 'biases': biases}
    _L0_conv_all = _L0_conv_setup()
    _L0_conv_in = {k: v for k, v in _L0_conv_all.items() if k in ('weights', 'biases')}
    del _L0_conv_all

    def _L1_conv_setup():
        import jax, jax.numpy as jnp
        import numpy as np
        key = jax.random.key(seed)
        W = jax.random.normal(key, (16, 16, 32, 32), dtype=jnp.float32)
        return {'W': W, 'num_iters': 5}
    _L1_conv_all = _L1_conv_setup()
    _L1_conv_in = {k: v for k, v in _L1_conv_all.items() if k in ()}
    del _L1_conv_all

    def _L2_conv_setup():
        import jax, jax.numpy as jnp
        import numpy as np
        K_SIZE = 3
        PAD = K_SIZE // 2

        def _diag_L(n, k):
            half = k // 2
            d = np.zeros(n, dtype=np.float32)
            d[:half] = 1.0
            d[n - half:] = 1.0
            if 2 * half < k:
                d[half] = 1.0
            return d

        def _circular_pad(w, H, W, k, p):
            w = jnp.roll(jnp.pad(jnp.flip(w, -1), ((0, 0), (0, 0), (0, 0), (0, W - k))), -p, axis=-1)
            w = jnp.roll(jnp.pad(jnp.flip(w, -2), ((0, 0), (0, 0), (0, H - k), (0, 0))), -p, axis=-2)
            return w
        key = jax.random.key(seed)
        kx, kw = jax.random.split(key)
        x = jax.random.normal(kx, (16, 16, 64, 64), dtype=jnp.float32)
        weight = jax.random.normal(kw, (16, 16, 3, 3), dtype=jnp.float32) * (2.0 / (16 * 9)) ** 0.5
        return {'x': x, 'weight': weight}
    _L2_conv_all = _L2_conv_setup()
    _L2_conv_in = {k: v for k, v in _L2_conv_all.items() if k in ('weight',)}
    del _L2_conv_all

    def _L3_conv_setup():
        import jax, jax.numpy as jnp
        import numpy as np
        KERNEL_SIZE = 3
        STRIDE = 1
        PADDING = 1
        key = jax.random.key(seed)
        k1, k2 = jax.random.split(key)
        x = jax.random.normal(k1, (16, 16, 128, 128), dtype=jnp.float32)
        K = jax.random.normal(k2, (3, 3, 16, 16), dtype=jnp.float32)
        return {'x': x, 'K': K}
    _L3_conv_all = _L3_conv_setup()
    _L3_conv_in = {k: v for k, v in _L3_conv_all.items() if k in ('K',)}
    del _L3_conv_all
    return {'x': x, 'L0_conv_weights': _L0_conv_in['weights'], 'L0_conv_biases': _L0_conv_in['biases'], 'L2_conv_weight': _L2_conv_in['weight'], 'L3_conv_K': _L3_conv_in['K']}

def reference(x, L0_conv_weights, L0_conv_biases, L2_conv_weight, L3_conv_K):
    import jax
    import jax.numpy as jnp

    def _L0_conv_ref(x, weights, biases):
        import jax, jax.numpy as jnp
        import numpy as np
        B, CIN, COUT, H, W = (16, 16, 16, 128, 128)
        KH, KW = (3, 3)
        STRIDE = 1
        PAD = 1
        out = jax.lax.conv_general_dilated(x, weights, window_strides=(STRIDE, STRIDE), padding=((PAD, PAD), (PAD, PAD)), dimension_numbers=('NCHW', 'OIHW', 'NCHW'))
        return out + biases[None, :, None, None]

    def _L1_conv_ref(W, num_iters):
        import jax, jax.numpy as jnp
        import numpy as np
        'Newton-Schulz iterative matrix inverse: X_{k+1} = X_k (2I - W X_k).\n\n            Init: X_0 = W^T / (||W||_1 * ||W||_inf), the classical convergent start.\n            W: [..., N, N] batched square matrices.\n            '
        n = W.shape[-1]
        absW = jnp.abs(W)
        norm1 = jnp.max(jnp.sum(absW, axis=-2), axis=-1)
        norminf = jnp.max(jnp.sum(absW, axis=-1), axis=-1)
        scale = (norm1 * norminf)[..., None, None]
        X = jnp.swapaxes(W, -1, -2) / scale
        two_I = 2.0 * jnp.eye(n, dtype=W.dtype)
        for _ in range(num_iters):
            X = jnp.matmul(X, two_I - jnp.matmul(W, X))
        return X

    def _L2_conv_ref(x, weight):
        import jax, jax.numpy as jnp
        import numpy as np
        K_SIZE = 3
        PAD = K_SIZE // 2

        def _diag_L(n, k):
            half = k // 2
            d = np.zeros(n, dtype=np.float32)
            d[:half] = 1.0
            d[n - half:] = 1.0
            if 2 * half < k:
                d[half] = 1.0
            return d

        def _circular_pad(w, H, W, k, p):
            w = jnp.roll(jnp.pad(jnp.flip(w, -1), ((0, 0), (0, 0), (0, 0), (0, W - k))), -p, axis=-1)
            w = jnp.roll(jnp.pad(jnp.flip(w, -2), ((0, 0), (0, 0), (0, H - k), (0, 0))), -p, axis=-2)
            return w
        B, Ci, H, W = x.shape
        k, p = (K_SIZE, PAD)
        w_pad = _circular_pad(weight, H, W, k, p)
        dL = jnp.asarray(np.outer(_diag_L(H, k), _diag_L(W, k)))
        Lw = jnp.fft.fft2(w_pad * dL)
        Kx = jnp.fft.ifft2(x, norm='ortho')
        z = jnp.einsum('oihw,bihw->bohw', Lw, Kx)
        y = jnp.fft.fft2(z, norm='ortho')
        return jnp.real(y).astype(x.dtype)

    def _L3_conv_ref(x, K):
        import jax, jax.numpy as jnp
        import numpy as np
        KERNEL_SIZE = 3
        STRIDE = 1
        PADDING = 1
        k = KERNEL_SIZE
        C = x.shape[1]
        O = K.shape[-1]
        Kw = K.reshape(k * k * C, O).reshape(C, k, k, O)
        Kw = jnp.transpose(Kw, (1, 2, 0, 3))
        y = jax.lax.conv_general_dilated(x, Kw, window_strides=(STRIDE, STRIDE), padding=[(PADDING, PADDING), (PADDING, PADDING)], dimension_numbers=('NCHW', 'HWIO', 'NCHW'))
        P = x.shape[-1] + 2 * PADDING
        n_loop = len(range(0, P - k, STRIDE))
        out_size = (P - k) // STRIDE + 1
        idx = jnp.arange(out_size)
        m = (idx < n_loop).astype(y.dtype)
        y = y * m[:, None] * m[None, :]
        return y

    def _gn(v, G=8, eps=1e-05):
        B_, C_, H_, W_ = v.shape
        g = v.reshape(B_, G, C_ // G, H_, W_)
        m = jnp.mean(g, axis=(2, 3, 4), keepdims=True)
        s = jnp.var(g, axis=(2, 3, 4), keepdims=True)
        return ((g - m) / jnp.sqrt(s + eps)).reshape(v.shape)

    def _ln_c(v, eps=1e-06):
        m = jnp.mean(v, axis=1, keepdims=True)
        s = jnp.var(v, axis=1, keepdims=True)
        return (v - m) / jnp.sqrt(s + eps)

    def _ln_t(v, eps=1e-05):
        m = jnp.mean(v, axis=-1, keepdims=True)
        s = jnp.var(v, axis=-1, keepdims=True)
        return (v - m) / jnp.sqrt(s + eps)

    def _to_tokens(v):
        B_, C_, H_, W_ = v.shape
        return v.reshape(B_, C_, H_ * W_).transpose(0, 2, 1)

    def _from_tokens(t, like):
        B_, C_, H_, W_ = like.shape
        return t.transpose(0, 2, 1).reshape(B_, C_, H_, W_)
    x = x + _L0_conv_ref(_gn(x), L0_conv_weights, L0_conv_biases)
    x = x + _L1_conv_ref(_gn(x), 5)
    x = x + _L2_conv_ref(_gn(x), L2_conv_weight)
    x = x + _L3_conv_ref(_gn(x), L3_conv_K)
    return x

_drawn_inputs = setup_inputs


def setup_inputs(seed=0):
    import zlib

    import numpy as np

    out = dict(_drawn_inputs(seed))
    spreads = {}
    factors = {}
    for name, (base, spread) in spreads.items():
        noise = np.random.default_rng([zlib.crc32(name.encode()), seed]).standard_normal(out[name].shape)
        drawn = base * np.exp(spread * noise) if base else spread * noise
        out[name] = jnp.asarray(drawn.astype(out[name].dtype))
    for name, factor in factors.items():
        out[name] = (out[name] * factor).astype(out[name].dtype)
    return out
```

```python
import concourse.bass as bass
import numpy as np
from concourse import mybir
from contextlib import ExitStack

B, C, H, W = 8, 16, 128, 128
G = 8
GC = C // G
EPS = 1e-5
TAPS = 3
WIN = 8
OUT_ROWS = WIN - TAPS + 1
NBLK = -(-H // OUT_ROWS)
LAST_ROW = H + 1 - WIN
OP = OUT_ROWS * C
FULL = (NBLK - 1) * OUT_ROWS
SPLIT_G = [(0, 4), (4, 4), (8, 4), (12, 4), (16, 4), (20, 2)]
NG = len(SPLIT_G)
WN = TAPS * OP
NMAT = 4
ROUNDS = C // (2 * NMAT)
STEPS = 5

K_IDENT = 0
K_SELM = K_IDENT + 128
K_SELL = K_SELM + 128
K_RES = K_SELL + 128
K_TAP = K_RES + WN
K_HOT = K_TAP + TAPS * OUT_ROWS
K_EDGE = K_HOT + G
K_ALL = K_EDGE + 4


def window_row(k):
    return OUT_ROWS * k - 1 if k < NBLK - 1 else LAST_ROW


def shape_constants():
    c = np.zeros((128, K_ALL), np.float32)
    q = np.arange(128)
    row, ch = q // C, q % C
    c[:, K_IDENT:K_IDENT + 128] = np.eye(128)
    same_group = (ch[:, None] // GC) == (ch[None, :] // GC)
    n = GC * H * W
    inner = (row >= 1) & (row <= OUT_ROWS)
    c[:, K_SELM:K_SELM + 128] = same_group * inner[:, None] * ((NBLK - 1) * W / n)
    only_last = inner & (LAST_ROW + row >= FULL)
    c[:, K_SELL:K_SELL + 128] = same_group * only_last[:, None] * (W / n)
    res = np.zeros((128, TAPS, OUT_ROWS, C), np.float32)
    for r in range(1, OUT_ROWS + 1):
        for k in range(C):
            res[r * C + k, 1, r - 1, k] = 1.0
    c[:, K_RES:K_RES + WN] = res.reshape(128, WN)
    tap = np.zeros((128, TAPS, OUT_ROWS), np.float32)
    for dy in range(TAPS):
        for r in range(OUT_ROWS):
            tap[(row == r + dy), dy, r] = 1.0
    c[:, K_TAP:K_TAP + TAPS * OUT_ROWS] = tap.reshape(128, -1)
    c[q, K_HOT + ch // GC] = 1.0
    c[:, K_EDGE + 0] = row != 0
    c[:, K_EDGE + 1] = row != WIN - 1
    c[:, K_EDGE + 2] = row == 0
    c[:, K_EDGE + 3] = row == WIN - 1
    return c


def at(per, b, n=0):
    return b * per + n


def wait(eng, sem, value):
    if isinstance(value, int) and value <= 0:
        return
    eng.wait_ge(sem, value)


def build(nc, x, w0, b0, w2, w3, consts, y):
    f32, f32r = mybir.dt.float32, mybir.dt.float32r
    ALU, ACT, AX = mybir.AluOpType, mybir.ActivationFunctionType, mybir.AxisListType
    ctx = ExitStack()
    with ctx:
        def sb(name, shape, dt=f32):
            return ctx.enter_context(nc.sbuf_tensor(name, shape, dt))

        def pb(name, shape):
            return ctx.enter_context(nc.psum_tensor(name, shape, f32))

        def sem(name):
            return ctx.enter_context(nc.semaphore(name))

        cst = sb("cst", [128, K_ALL])
        ident = cst[:, K_IDENT:K_IDENT + 128]
        sel_main = cst[:, K_SELM:K_SELM + 128]
        sel_last = cst[:, K_SELL:K_SELL + 128]
        residual = cst[:, K_RES:K_RES + WN]
        tap_mask = cst[:, K_TAP:K_TAP + TAPS * OUT_ROWS].rearrange("p (d r) -> p d r", d=TAPS)
        onehot = cst[:, K_HOT:K_HOT + G]
        edge_keep = cst[:, K_EDGE:K_EDGE + 2]
        edge_drop = cst[:, K_EDGE + 2:K_EDGE + 4]
        ones_mean = sb("ones_mean", [128, 128])
        ones_var = sb("ones_var", [128, 128])
        ones_all = sb("ones_all", [128, 128])

        s_cst = sem("s_cst")
        s_wld = sem("s_wld")
        s_init = sem("s_init")
        s_pads = sem("s_pads")
        s_zero = sem("s_zero")
        s_toep = sem("s_toep")

        class Conv:

            def __init__(self, name, weights):
                self.name = name
                self.weights = weights
                self.win = sb(f"win_{name}", [128, NBLK, W])
                self.d = sb(f"d_{name}", [128, 2, NBLK, W + 2], f32r)
                self.out = sb(f"out_{name}", [OP, NBLK, W])
                self.compact = sb(f"compact_{name}", [128, TAPS, TAPS, C])
                self.base = sb(f"base_{name}", [128, WN])
                self.scaled = sb(f"scaled_{name}", [128, WN])
                self.w = sb(f"w_{name}", [128, 2, WN], f32r)
                self.col = sb(f"col_{name}", [128, 16])
                self.mv = sb(f"mv_{name}", [128, 2, 2])
                self.bn = sb(f"bn_{name}", [128, NBLK // 3 + 1, 6])
                self.s_win = sem(f"win_{name}_loaded")
                self.s_stat = sem(f"stat_{name}_ready")
                self.s_sum = sem(f"sum_{name}_ready")
                self.s_ve = sem(f"var_{name}_ready")
                self.s_sd = sem(f"sqrt_{name}_ready")
                self.s_fix = sem(f"win_{name}_fixed")
                self.s_w = sem(f"w_{name}_ready")
                self.s_dh = sem(f"dh_{name}_ready")
                self.s_dl = sem(f"dl_{name}_ready")
                self.s_acc = sem(f"acc_{name}_ready")
                self.s_out = sem(f"out_{name}_ready")
                self.s_chain = sem(f"chain_{name}")
                self.s_sent = sem(f"out_{name}_sent")

        cA, cC, cD = Conv("A", w0), Conv("C", w2), Conv("D", w3)
        s_pad = sem("pad_C_ready")
        bias = sb("bias", [OP, 1])

        xN = sb("xN", [H, C, W])
        DN = sb("DN", [H, C, W])
        st = sb("st", [128, G, 6])
        dev = sb("dev", [128, 2, G * 2])
        tB = sb("tB", [128, 6, G])
        tC = sb("tC", [128, 6, G])
        pick = sb("pick", [128, 2, G])
        R = [[sb(f"R{s}{j}", [128, NMAT, 128]) for j in range(2)] for s in range(2)]
        V = [sb(f"V{s}", [128, NMAT, 128]) for s in range(2)]
        U = [sb(f"U{s}", [128, NMAT, 128]) for s in range(2)]
        NC2 = 2 * NMAT
        sums = sb("sums", [128, 2, NC2])
        top = sb("top", [2 * NC2, 1])
        diag = sb("diag", [2 * NC2, 2 * NC2])
        norms = sb("norms", [128, 2, NC2])
        scl = sb("scl", [128, 4, NC2])

        conv_ps = [pb(f"conv_ps{i}", [128, 4, W]) for i in range(2)]
        R_ps = [pb(f"R_ps{s}", [128, NMAT, 128]) for s in range(2)]
        V_ps = [pb(f"V_ps{s}", [128, NMAT, 128]) for s in range(2)]
        win_ps = pb("win_ps", [128, 512])
        row_ps = pb("row_ps", [128, 512])

        s_x1 = sem("x1_rows_loaded")
        sB_bn, sB_sum, sB_ve, sB_sd, sB_ready = (sem(f"rows_B_{n}") for n in ("stat", "sum", "var", "sqrt", "ready"))
        sC_bn, sC_sum, sC_ve, sC_sd, sC_ready = (sem(f"rows_C_{n}") for n in ("stat", "sum", "var", "sqrt", "ready"))
        s_chainB = sem("chain_B")
        s_chainC = sem("chain_rows_C")
        s_DN = sem("DN_ready")
        s_T = sem("transposed")
        s_Gr = sem("gram_ready")
        s_V0 = sem("V0_ready")
        s_abs = sem("abs_sums_ready")
        s_nT = sem("norms_transposed")
        s_dg = sem("diag_ready")
        s_nB = sem("norms_spread")
        s_sc = sem("scales_ready")
        s_V0s = sem("V0_scaled")
        s_R0 = sem("R0_ready")
        s_Rp = sem("R_product")
        s_Vp = sem("V_product")
        s_R = sem("R_ready")
        s_V = sem("V_ready")
        s_U = sem("U_ready")
        s_x2 = sem("x2_ready")
        s_ycol = sem("y_column_ready")
        s_y = sem("y_stored")

        block = ctx.enter_context(nc.Block())

        n_x = NBLK
        n_x1 = NBLK
        n_x2 = NBLK + 2
        n_x3 = 5
        n_y = NBLK + 1

        def load_x(sp, b):
            wait(sp, cA.s_dl, at(NG, b))
            for k in range(NBLK):
                h0 = window_row(k)
                lo, hi = max(h0, 0), min(h0 + WIN, H)
                sp.dma_start(cA.win[(lo - h0) * C:(hi - h0) * C, k, :],
                             x[bass.ds(b, 1), :, lo:hi, :].rearrange("b c h w -> (b h) c w"))\
                    .then_inc(cA.s_win, 16)

        def rows_from_windows(sp, b):
            wait(sp, cC.s_win, at(16 * n_x2, b))
            for g, (k0, kn) in enumerate(SPLIT_G):
                wait(sp, cA.s_out, at(NG, b, g + 1))
                for k in range(k0, k0 + kn):
                    if k < NBLK - 1:
                        sp.dma_start(xN[OUT_ROWS * k:OUT_ROWS * (k + 1), :, :], cA.out[:, k, :])\
                            .then_inc(s_x1, 16)
                    else:
                        first = FULL - (LAST_ROW + 1)
                        sp.dma_start(xN[FULL:H, :, :], cA.out[first * C:OP, k, :]).then_inc(s_x1, 16)

        def windows_from_rows(sp, b):
            wait(sp, cC.s_dl, at(NG, b))
            wait(sp, s_x2, at(2 * ROUNDS, b, 2 * ROUNDS))
            for k in range(NBLK):
                h0 = window_row(k)
                lo, hi = max(h0, 0), min(h0 + WIN, H)
                sp.dma_start(cC.win[(lo - h0) * C:(hi - h0) * C, k, :], xN[lo:hi, :, :])\
                    .then_inc(cC.s_win, 16)
            sp.dma_start(cC.win[0:C, 0, :], xN[H - 1:H, :, :]).then_inc(cC.s_win, 16)
            sp.dma_start(cC.win[(WIN - 1) * C:, NBLK - 1, :], xN[0:1, :, :]).then_inc(cC.s_win, 16)

        def windows_from_windows(sp, b):
            wait(sp, cC.s_out, at(NG, b, NG))
            wait(sp, cD.s_dl, at(NG, b))
            o, w, last = cC.out, cD.win, NBLK - 1
            above = window_row(last) - OUT_ROWS * (last - 1)
            below = OUT_ROWS * last - (LAST_ROW + 1)
            sp.dma_start(w[C:C + OP, :, :], o[:, :, :]).then_inc(cD.s_win, 16)
            sp.dma_start(w[0:C, 1:last, :], o[OP - C:OP, 0:last - 1, :]).then_inc(cD.s_win, 16)
            sp.dma_start(w[0:C, last, :], o[above * C:(above + 1) * C, last - 1, :]).then_inc(cD.s_win, 16)
            sp.dma_start(w[(WIN - 1) * C:, 0:last - 1, :], o[0:C, 1:last, :]).then_inc(cD.s_win, 16)
            sp.dma_start(w[(WIN - 1) * C:, last - 1, :], o[below * C:(below + 1) * C, last, :])\
                .then_inc(cD.s_win, 16)

        def store_y(sp, b):
            def rows(lo, hi):
                return y[bass.ds(b, 1), :, lo:hi, :].rearrange("b c h w -> (b h) c w")
            wait(sp, s_ycol, at(1, b, 1))
            sp.dma_start(rows(H - 1, H), cC.out[OP - C:OP, NBLK - 1, :]).then_inc(s_y, 16)
            for g, (k0, kn) in enumerate(SPLIT_G):
                wait(sp, cD.s_out, at(NG, b, g + 1))
                for k in reversed(range(k0, k0 + kn)):
                    if k < NBLK - 1:
                        sp.dma_start(rows(OUT_ROWS * k, OUT_ROWS * (k + 1)), cD.out[:, k, :]).then_inc(s_y, 16)
                    else:
                        first = FULL - (LAST_ROW + 1)
                        sp.dma_start(rows(FULL, H - 1), cD.out[first * C:OP - C, k, :]).then_inc(s_y, 16)

        def newton(dve, link, inv, ve, sd, t1, t2):
            link(dve.reciprocal(t1, sd))
            link(dve.tensor_tensor(t2, t1, t1, ALU.mult))
            link(dve.tensor_tensor(t2, t2, ve, ALU.mult))
            link(dve.tensor_scalar(t2, t2, -0.5, 1.5, ALU.mult, ALU.add))
            link(dve.tensor_tensor(inv, t1, t2, ALU.mult))

        class Chain:

            def __init__(self, eng, s, per, b, done=0):
                self.eng, self.s, self.per, self.b, self.n = eng, s, per, b, done

            def __call__(self, ins):
                self.n += 1
                ins.then_inc(self.s, 1)
                self.eng.wait_ge(self.s, at(self.per, self.b, self.n))

        MEAN, NEG, VE, SD, T1, T2, INV, OUTB, DEV, ADD, SPARE = 0, 1, 2, 3, 4, 5, 6, 7, 8, 10, 12

        def col(c, j, n=1, rows=128):
            return c.col[0:rows, j:j + n]

        NWIN = 1 + 6 + 5 + 2

        def win_stats_1(dve, c, b):
            link = Chain(dve, c.s_chain, NWIN, b)
            dve.wait_ge(c.s_win, at(16 * (n_x if c is cA else n_x3), b, 16 * (n_x if c is cA else n_x3)))
            for j in range(NBLK // 3):
                dve.bn_stats(c.bn[:, j, :], c.win[:, 3 * j:3 * j + 3, :])
            link(dve.bn_stats(c.bn[:, NBLK // 3, :], c.win[:, NBLK - 1, :]))
            dve.memset(col(c, SPARE), 0.0)
            dve.bn_aggr(c.mv[:, 0, :], c.bn[:, 0:NBLK // 3, :])
            dve.bn_aggr(c.mv[:, 1, :], c.bn[:, NBLK // 3, :]).then_inc(c.s_stat, 1)
            return link

        def win_stats_2(dve, c, b):
            link = Chain(dve, c.s_chain, NWIN, b, 1)
            dve.wait_ge(c.s_sum, at(2, b, 1))
            link(dve.tensor_copy(col(c, MEAN), win_ps[:, 0:1]))
            link(dve.tensor_scalar(col(c, DEV, 2), c.mv[:, :, 0], col(c, MEAN), None, ALU.subtract))
            link(dve.tensor_tensor(col(c, DEV, 2), col(c, DEV, 2), col(c, DEV, 2), ALU.mult))
            dve.tensor_tensor(col(c, DEV, 2), col(c, DEV, 2), c.mv[:, :, 1], ALU.add).then_inc(c.s_stat, 1)
            link(dve.tensor_scalar(col(c, ADD, 2), edge_drop, col(c, MEAN), None, ALU.mult))
            link(dve.tensor_scalar(col(c, NEG), col(c, MEAN), -1.0, None, ALU.mult))
            dve.tensor_scalar(c.win[:, 0, :], c.win[:, 0, :], edge_keep[:, 0:1], col(c, ADD),
                              ALU.mult, ALU.add)
            if c is cA:
                link(dve.tensor_tensor(col(c, OUTB, rows=OP), col(c, MEAN, rows=OP), bias[:, :], ALU.add))
            else:
                link(dve.tensor_copy(col(c, OUTB), col(c, MEAN)))
            dve.tensor_scalar(c.win[:, NBLK - 1, :], c.win[:, NBLK - 1, :], edge_keep[:, 1:2],
                              col(c, ADD + 1), ALU.mult, ALU.add).then_inc(c.s_fix, 1)

        def win_stats_3(dve, c, b):
            link = Chain(dve, c.s_chain, NWIN, b, 7)
            dve.wait_ge(c.s_sum, at(2, b, 2))
            dve.tensor_scalar(col(c, VE), win_ps[:, 1:2], EPS, None, ALU.add).then_inc(c.s_ve, 1)
            dve.wait_ge(c.s_sd, at(1, b, 1))
            newton(dve, link, col(c, INV), col(c, VE), col(c, SD), col(c, T1), col(c, T2))
            conv_weights(dve, link, c, b, col(c, INV))

        def conv_weights(dve, link, c, b, inv):
            wait(dve, c.s_acc, at(NG, b))
            link(dve.scalar_tensor_tensor(c.scaled[:, :], c.base[:, :], inv, residual, ALU.mult, ALU.add))
            link(dve.tensor_copy(c.w[:, 0, :], c.scaled[:, :]))
            dve.tensor_tensor(c.w[:, 1, :], c.scaled[:, :], c.w[:, 0, :].bitcast(f32), ALU.subtract)\
                .then_inc(c.s_w, 1)

        def low_parts(dve, c, b, g):
            k0, kn = SPLIT_G[g]
            dve.wait_ge(c.s_dh, at(NG, b, g + 1))
            dve.scalar_tensor_tensor(c.d[:, 1, k0:k0 + kn, 1:W + 1], c.win[:, k0:k0 + kn, :], col(c, MEAN),
                                     c.d[:, 0, k0:k0 + kn, 1:W + 1].bitcast(f32),
                                     ALU.subtract, ALU.subtract).then_inc(c.s_dl, 1)

        def high_parts(act, c, b, g):
            k0, kn = SPLIT_G[g]
            if g == 0:
                act.wait_ge(c.s_fix, at(1, b, 1))
                wait(act, c.s_acc, at(NG, b))
                if c is cC:
                    act.wait_ge(c.s_win, at(16 * n_x2, b, 16 * n_x2))
            act.activation(c.d[:, 0, k0:k0 + kn, 1:W + 1], c.win[:, k0:k0 + kn, :], ACT.Identity,
                           bias=col(c, NEG)).then_inc(c.s_dh, 1)

        def win_mean(pe, c, b):
            pe.wait_ge(c.s_stat, at(2, b, 1))
            pe.matmul(win_ps[:, 0:1], sel_main, c.mv[:, 0, 0:1], start=True, stop=False)
            pe.matmul(win_ps[:, 0:1], sel_last, c.mv[:, 1, 0:1], start=False, stop=True).then_inc(c.s_sum, 1)

        def win_var(pe, c, b):
            pe.wait_ge(c.s_stat, at(2, b, 2))
            pe.matmul(win_ps[:, 1:2], sel_main, col(c, DEV), start=True, stop=False)
            pe.matmul(win_ps[:, 1:2], sel_last, col(c, DEV + 1), start=False, stop=True).then_inc(c.s_sum, 1)

        NROW = 4 + 5

        def row_stats(dve, s_bn, s_sum, s_ve, s_sd, chain, per, t, b, ready):
            link = Chain(dve, chain, per, b)
            mean, inv, ve, sd, t1, t2 = (t[:, j, :] for j in range(6))
            for g in range(G):
                ins = dve.bn_stats(st[:, g, :], xN[:, GC * g:GC * (g + 1), :])
            ins.then_inc(s_bn, 1)
            halves = st[:, :, :].rearrange("p g (a t) -> p (g a) t", t=3)
            dve.wait_ge(s_bn, at(2, b, 1))
            dve.wait_ge(s_sum, at(2, b, 1))
            link(dve.tensor_reduce(mean, row_ps[:, 0:2 * G].rearrange("p (g a) -> p g a", a=2), AX.X, ALU.add))
            d, sq = dev[:, 0, :], dev[:, 1, :]
            link(dve.tensor_tensor(d.rearrange("p (g a) -> p g a", a=2),
                                   halves[:, :, 1].rearrange("p (g a) -> p g a", a=2),
                                   mean.unsqueeze(2).broadcast_to([128, G, 2]), ALU.subtract))
            link(dve.scalar_tensor_tensor(sq, d, float(GC * W // 2), d, ALU.mult, ALU.mult))
            dve.tensor_tensor(sq, sq, halves[:, :, 2], ALU.add).then_inc(s_bn, 1)
            dve.wait_ge(s_sum, at(2, b, 2))
            link(dve.tensor_reduce(t1, row_ps[:, 2 * G:4 * G].rearrange("p (g a) -> p g a", a=2), AX.X, ALU.add))
            dve.tensor_scalar(ve, t1, EPS, None, ALU.add).then_inc(s_ve, 1)
            dve.wait_ge(s_sd, at(1, b, 1))
            newton(dve, link, inv, ve, sd, t1, t2)
            return link

        def row_mean(pe, s_bn, s_sum, b):
            pe.wait_ge(s_bn, at(2, b, 1))
            pe.matmul(row_ps[:, 0:2 * G], ones_mean[:, :],
                      st[:, :, :].rearrange("p g (a t) -> p (g a) t", t=3)[:, :, 1],
                      start=True, stop=True).then_inc(s_sum, 1)

        def row_var(pe, s_bn, s_sum, b):
            pe.wait_ge(s_bn, at(2, b, 2))
            pe.matmul(row_ps[:, 2 * G:4 * G], ones_var[:, :], dev[:, 1, :], start=True, stop=True)\
                .then_inc(s_sum, 1)

        def conv_group(pe, c, b, g, prev):
            k0, kn = SPLIT_G[g]
            if g == 0:
                pe.wait_ge(c.s_w, at(1, b, 1))
            pe.wait_ge(c.s_dl, at(NG, b, g + 1))
            if c is cC:
                pe.wait_ge(s_pad, at(NG, b, g + 1))
            if g >= 2:
                pe.wait_ge(c.s_out, at(NG, b, g - 1))
            elif prev is not None:
                pe.wait_ge(prev[0].s_out, at(NG, prev[1], NG - 1 + g))
            n = 0
            for dx in range(TAPS):
                for wp, dp in ((0, 0), (0, 1), (1, 0)):
                    ins = pe.matmul(conv_ps[g % 2][0:OP, 0:kn, :], c.w[:, wp, dx * OP:(dx + 1) * OP],
                                    c.d[:, dp, k0:k0 + kn, dx:dx + W], start=n == 0, stop=n == 8)
                    n += 1
            ins.then_inc(c.s_acc, 1)

        def conv_out(act, c, b, g):
            k0, kn = SPLIT_G[g]
            act.wait_ge(c.s_acc, at(NG, b, g + 1))
            if g == 0:
                if c is cA:
                    wait(act, s_x1, at(16 * n_x1, b))
                if c is cC:
                    wait(act, cD.s_win, at(16 * n_x3, b))
                    wait(act, s_ycol, at(1, b))
                if c is cC or c is cD:
                    wait(act, s_y, at(16 * n_y, b))
            wn = W - 1 if c is cD else W
            act.activation(c.out[:, k0:k0 + kn, 0:wn], conv_ps[g % 2][0:OP, 0:kn, 0:wn], ACT.Identity,
                           bias=col(c, OUTB, rows=OP)).then_inc(c.s_out, 1)

        NCHK = 2 * ROUNDS
        per_R = NCHK * (STEPS - 1)
        per_V = NCHK * (STEPS - 1)
        per_Vp = NCHK * STEPS

        def sp_cycle(sp, i, cd, ab, pre):
            if ab:
                rows_from_windows(sp, i + 1)
            if pre:
                load_x(sp, i + 2)
            if cd:
                windows_from_windows(sp, i)
            if ab:
                windows_from_rows(sp, i + 1)
            if cd:
                store_y(sp, i)

        def pe_round(pe, b, r, c, cb):
            for s in range(2):
                ch = 2 * r + s
                pe.wait_ge(s_DN, at(NCHK, b, ch + 1))
                if r > 0:
                    pe.wait_ge(s_x2, at(NCHK, b, ch - 1))
                for m in range(NMAT):
                    ins = pe.transpose(V_ps[s][:, m, :], DN[:, NMAT * ch + m, :], ident)
                ins.then_inc(s_T, 1)
            for s in range(2):
                ch = 2 * r + s
                for m in range(NMAT):
                    ins = pe.matmul(R_ps[s][:, m, :], DN[:, NMAT * ch + m, :], DN[:, NMAT * ch + m, :],
                                    start=True, stop=True)
                ins.then_inc(s_Gr, 1)
            if c is not None:
                win_mean(pe, c, cb)
            pe.wait_ge(s_abs, at(ROUNDS, b, r + 1))
            pe.transpose(row_ps[0:2 * NC2, 128:256], sums[:, :, :].rearrange("p a c -> p (a c)"), ident)\
                .then_inc(s_nT, 1)
            pe.wait_ge(s_dg, at(ROUNDS, b, r + 1))
            pe.matmul(row_ps[:, 256:256 + 2 * NC2], ones_all[0:2 * NC2, :], diag[:, :], start=True, stop=True)\
                .then_inc(s_nB, 1)
            for k in range(STEPS):
                for s in range(2):
                    ch = 2 * r + s
                    Rk = R[s][k % 2]
                    if k == 0:
                        pe.wait_ge(s_R0, at(NCHK, b, ch + 1))
                        pe.wait_ge(s_V0, at(NCHK, b, ch + 1))
                    else:
                        pe.wait_ge(s_R, at(per_R, b, 2 * (STEPS - 1) * r + 2 * (k - 1) + s + 1))
                    if k < STEPS - 1:
                        for m in range(NMAT):
                            ins = pe.matmul(R_ps[s][:, m, :], Rk[:, m, :], Rk[:, m, :], start=True, stop=True)
                        ins.then_inc(s_Rp, 1)
                    if k > 0:
                        pe.wait_ge(s_V, at(per_V, b, 2 * (STEPS - 1) * r + 2 * (k - 1) + s + 1))
                    for m in range(NMAT):
                        ins = pe.matmul(V_ps[s][:, m, :], Rk[:, m, :], V[s][:, m, :], start=True, stop=True)
                    ins.then_inc(s_Vp, 1)
                if k == 0 and c is not None:
                    win_var(pe, c, cb)

        def pe_cycle(pe, i, cd, ab, pre, prevA, prevC):
            if ab:
                for g in range(NG):
                    conv_group(pe, cA, i + 1, g, prevA)
            if cd:
                for g in range(NG):
                    conv_group(pe, cC, i, g, prevC)
            if ab:
                row_mean(pe, sB_bn, sB_sum, i + 1)
                row_var(pe, sB_bn, sB_sum, i + 1)
                pe_round(pe, i + 1, 0, cA if pre else None, i + 2)
                pe_round(pe, i + 1, 1, cD if cd else None, i)
            elif cd:
                win_mean(pe, cD, i)
                win_var(pe, cD, i)
            for g in range(NG):
                if cd:
                    conv_group(pe, cD, i, g, (cC, i))
                if ab and g == 3:
                    row_mean(pe, sC_bn, sC_sum, i + 1)
                if ab and g == 4:
                    row_var(pe, sC_bn, sC_sum, i + 1)

        def act_sqrt(act, s_ve, s_sd, out, in_, b):
            act.wait_ge(s_ve, at(1, b, 1))
            act.activation(out, in_, ACT.Sqrt).then_inc(s_sd, 1)

        def act_round(act, b, r, c, cb):
            for s in range(2):
                ch = 2 * r + s
                act.wait_ge(s_T, at(NCHK, b, ch + 1))
                act.activation(V[s][:, :, :], V_ps[s][:, :, :], ACT.Copy).then_inc(s_V0, 1)
            for k in range(STEPS - 1):
                for s in range(2):
                    act.wait_ge(s_Rp, at(per_R, b, 2 * (STEPS - 1) * r + 2 * k + s + 1))
                    if k > 0:
                        act.wait_ge(s_Vp, at(per_Vp, b, 2 * STEPS * r + 2 * (k - 1) + s + 1))
                    act.activation(R[s][(k + 1) % 2][:, :, :], R_ps[s][:, :, :], ACT.Copy).then_inc(s_R, 1)
                if c is not None:
                    high_parts(act, c, cb, k)
                    if k == 0:
                        act_sqrt(act, c.s_ve, c.s_sd, col(c, SD), col(c, VE), cb)
            if c is not None:
                for g in range(STEPS - 1, NG):
                    high_parts(act, c, cb, g)

        def act_cycle(act, i, cd, ab, pre):
            if ab:
                for g in range(NG):
                    conv_out(act, cA, i + 1, g)
            if cd:
                for g in range(NG):
                    conv_out(act, cC, i, g)
            if ab:
                act_sqrt(act, sB_ve, sB_sd, tB[:, 3, :], tB[:, 2, :], i + 1)
                act_round(act, i + 1, 0, cA if pre else None, i + 2)
                act_round(act, i + 1, 1, cD if cd else None, i)
            elif cd:
                act_sqrt(act, cD.s_ve, cD.s_sd, col(cD, SD), col(cD, VE), i)
                for g in range(NG):
                    high_parts(act, cD, i, g)
            for g in range(NG):
                if cd:
                    conv_out(act, cD, i, g)
                if ab and g == 4:
                    act_sqrt(act, sC_ve, sC_sd, tC[:, 3, :], tC[:, 2, :], i + 1)
            if ab:
                for g in range(NG):
                    high_parts(act, cC, i + 1, g)

        perRC = NROW + 4 + 2
        NRND = 6
        NROW_B = NROW + 1
        perB = NROW_B + ROUNDS * NRND

        def dve_round(dve, b, r, c, cb):
            link = Chain(dve, s_chainB, perB, b, NROW_B + r * NRND)
            for s in range(2):
                ch = 2 * r + s
                dve.wait_ge(s_DN, at(NCHK, b, ch + 1))
                dve.tensor_reduce(sums[:, 0, NMAT * s:NMAT * (s + 1)], DN[:, NMAT * ch:NMAT * (ch + 1), :],
                                  AX.X, ALU.add, apply_absolute_value=True)
            for s in range(2):
                ch = 2 * r + s
                dve.wait_ge(s_V0, at(NCHK, b, ch + 1))
                ins = dve.tensor_reduce(sums[:, 1, NMAT * s:NMAT * (s + 1)], V[s][:, :, :],
                                        AX.X, ALU.add, apply_absolute_value=True)
            ins.then_inc(s_abs, 1)
            if c is not None:
                win_stats_1(dve, c, cb)
            dve.wait_ge(s_nT, at(ROUNDS, b, r + 1))
            link(dve.tensor_reduce(top[:, :], row_ps[0:2 * NC2, 128:256], AX.X, ALU.max))
            dve.tensor_scalar(diag[:, :], ident[0:2 * NC2, 0:2 * NC2], top[:, :], None, ALU.mult)\
                .then_inc(s_dg, 1)
            if c is not None:
                win_stats_2(dve, c, cb)
            dve.wait_ge(s_nB, at(ROUNDS, b, r + 1))
            link(dve.tensor_copy(norms[:, :, :].rearrange("p a c -> p (a c)"), row_ps[:, 256:256 + 2 * NC2]))
            link(dve.tensor_tensor(scl[:, 0, :], norms[:, 0, :], norms[:, 1, :], ALU.mult))
            link(dve.reciprocal(scl[:, 1, :], scl[:, 0, :]))
            link(dve.tensor_scalar(scl[:, 2, :], scl[:, 1, :], -1.0, None, ALU.mult))
            g0 = r * NC2 // GC
            link(dve.tensor_tensor(scl[:, 3, :].rearrange("p (g a) -> p g a", a=GC),
                                   scl[:, 1, :].rearrange("p (g a) -> p g a", a=GC),
                                   tB[:, 4, g0:g0 + NC2 // GC].unsqueeze(2).broadcast_to([128, NC2 // GC, GC]),
                                   ALU.mult))
            for s in range(2):
                ch = 2 * r + s
                dve.wait_ge(s_Gr, at(NCHK, b, ch + 1))
                for m in range(NMAT):
                    ins = dve.scalar_tensor_tensor(R[s][0][:, m, :], R_ps[s][:, m, :],
                                                   scl[:, 2, NMAT * s + m:NMAT * s + m + 1], ident,
                                                   ALU.mult, ALU.add)
                ins.then_inc(s_R0, 1)
            for k in range(STEPS):
                for s in range(2):
                    ch = 2 * r + s
                    dve.wait_ge(s_Vp, at(per_Vp, b, 2 * STEPS * r + 2 * k + s + 1))
                    if k == 0:
                        dve.wait_ge(s_V0s, at(NCHK, b, ch + 1))
                        for m in range(NMAT):
                            ins = dve.scalar_tensor_tensor(V[s][:, m, :], V_ps[s][:, m, :],
                                                           scl[:, 3, NMAT * s + m:NMAT * s + m + 1],
                                                           U[s][:, m, :], ALU.mult, ALU.add)
                        ins.then_inc(s_V, 1)
                    elif k < STEPS - 1:
                        dve.wait_ge(s_V, at(per_V, b, 2 * (STEPS - 1) * r + 2 * (k - 1) + s + 1))
                        dve.tensor_tensor(V[s][:, :, :], V_ps[s][:, :, :], V[s][:, :, :], ALU.add)\
                            .then_inc(s_V, 1)
                    else:
                        dve.wait_ge(s_U, at(NCHK, b, ch + 1))
                        dve.tensor_tensor(xN[:, NMAT * ch:NMAT * (ch + 1), :], V_ps[s][:, :, :],
                                          U[s][:, :, :], ALU.add).then_inc(s_x2, 1)
                if c is not None:
                    if k == 0:
                        win_stats_3(dve, c, cb)
                    else:
                        low_parts(dve, c, cb, k - 1)
            if c is not None:
                for g in range(STEPS - 1, NG):
                    low_parts(dve, c, cb, g)

        def dve_cycle(dve, i, cd, ab, pre):
            if ab:
                b = i + 1
                dve.wait_ge(s_x1, at(16 * n_x1, b, 16 * n_x1))
                link = row_stats(dve, sB_bn, sB_sum, sB_ve, sB_sd, s_chainB, perB, tB, b, sB_ready)
                link(dve.tensor_tensor(tB[:, 4, :], tB[:, 2, :], tB[:, 1, :], ALU.mult))
                assert link.n == NROW_B, link.n
                dve_round(dve, b, 0, cA if pre else None, i + 2)
                dve_round(dve, b, 1, cD if cd else None, i)
            elif cd:
                win_stats_1(dve, cD, i)
                win_stats_2(dve, cD, i)
                win_stats_3(dve, cD, i)
                for g in range(NG):
                    low_parts(dve, cD, i, g)
            if ab:
                dve.wait_ge(s_x2, at(NCHK, b, NCHK))
                link = row_stats(dve, sC_bn, sC_sum, sC_ve, sC_sd, s_chainC, perRC, tC, b, sC_ready)
                link(dve.tensor_tensor(pick[:, :, :], tC[:, 0:2, :],
                                       onehot.unsqueeze(1).broadcast_to([128, 2, G]), ALU.mult))
                link(dve.tensor_reduce(col(cC, MEAN), pick[:, 0, :], AX.X, ALU.add))
                link(dve.tensor_reduce(col(cC, INV), pick[:, 1, :], AX.X, ALU.add))
                link(dve.tensor_copy(col(cC, OUTB), col(cC, MEAN)))
                dve.tensor_scalar(col(cC, NEG), col(cC, MEAN), -1.0, None, ALU.mult).then_inc(cC.s_fix, 1)
                conv_weights(dve, link, cC, b, col(cC, INV))
                assert link.n == perRC, link.n
                for g in range(NG):
                    low_parts(dve, cC, b, g)

        def copy_column(pool, out, in_):
            p, *n = out.shape
            ones = ones_all[0:p, 0:int(np.prod(n))]
            if len(n) == 3:
                ones = ones.rearrange("p (a k o) -> p a k o", a=n[0], o=1)
            else:
                ones = ones.unsqueeze(2)
            return pool.tensor_tensor(out, in_, ones, ALU.mult)

        def pool_cycle(pool, i, cd, ab, pre):
            if ab:
                b = i + 1
                pool.wait_ge(sB_bn, at(2, b, 2))
                wait(pool, s_x2, at(NCHK, b))
                for ch in range(NCHK):
                    gs = slice(ch * NMAT // GC, (ch + 1) * NMAT // GC)
                    pool.tensor_tensor(
                        DN[:, NMAT * ch:NMAT * (ch + 1), :].rearrange("p (g a) w -> p g (a w)", a=GC),
                        xN[:, NMAT * ch:NMAT * (ch + 1), :].rearrange("p (g a) w -> p g (a w)", a=GC),
                        tB[:, 0, gs].unsqueeze(2).broadcast_to([128, NMAT // GC, GC * W]),
                        ALU.subtract).then_inc(s_DN, 1)
                for r in range(ROUNDS):
                    for s in range(2):
                        pool.wait_ge(s_R0, at(NCHK, b, 2 * r + 1))
                        pool.tensor_tensor(U[s][:, :, :], V[s][:, :, :],
                                           scl[:, 3, NMAT * s:NMAT * (s + 1)].unsqueeze(2)
                                           .broadcast_to([128, NMAT, 128]), ALU.mult).then_inc(s_V0s, 1)
                    for s in range(2):
                        ch = 2 * r + s
                        pool.wait_ge(s_V, at(per_V, b, 2 * (STEPS - 1) * r + 2 * (STEPS - 2) + s + 1))
                        pool.tensor_tensor(U[s][:, :, :], V[s][:, :, :], xN[:, NMAT * ch:NMAT * (ch + 1), :],
                                           ALU.add).then_inc(s_U, 1)
                    if r == 1 and cd:
                        y_column(pool, i)
                for g, (k0, kn) in enumerate(SPLIT_G):
                    pool.wait_ge(cC.s_dl, at(NG, b, g + 1))
                    d = cC.d[:, :, k0:k0 + kn, :]
                    copy_column(pool, d[:, :, :, 0:1], d[:, :, :, W:W + 1].bitcast(f32))
                    copy_column(pool, d[:, :, :, W + 1:W + 2], d[:, :, :, 1:2].bitcast(f32)).then_inc(s_pad, 1)
            elif cd:
                y_column(pool, i)

        def y_column(pool, i):
            pool.wait_ge(cC.s_out, at(NG, i, NG))
            wait(pool, s_y, at(16 * n_y, i))
            copy_column(pool, cD.out[:, :, W - 1:W], cC.out[:, :, W - 1:W]).then_inc(s_ycol, 1)

        n_wld = 3 * WIN + OUT_ROWS

        @block.sync
        def _(sp):
            sp.dma_start(cst[:, :], consts).then_inc(s_cst, 16)
            sp.wait_ge(s_zero, 1)
            load_x(sp, 0)
            for j in range(OUT_ROWS):
                sp.dma_start(bias[j * C:(j + 1) * C, :], b0.rearrange("(c a) -> c a", a=1)).then_inc(s_wld, 16)
            for c in (cA, cC, cD):
                for j in range(WIN):
                    sp.dma_start(c.compact[j * C:(j + 1) * C, :, :, :], c.weights).then_inc(s_wld, 16)
            load_x(sp, 1)
            sp_cycle(sp, -1, False, True, False)
            sp_cycle(sp, 0, True, True, True)
            with sp.Fori(1, B - 2) as i:
                sp_cycle(sp, i, True, True, True)
            sp_cycle(sp, B - 2, True, True, False)
            sp_cycle(sp, B - 1, True, False, False)
            sp.wait_ge(s_y, 16 * n_y * B)

        @block.gpsimd
        def _(pool):
            pool.memset(ones_mean[:, :], 1.0 / (GC * W)).then_inc(s_init, 1)
            pool.memset(ones_var[:, :], 1.0 / (GC * H * W)).then_inc(s_init, 1)
            pool.memset(ones_all[:, :], 1.0).then_inc(s_init, 1)
            for c in (cA, cD):
                pool.memset(c.d[:, :, :, 0:1].bitcast(f32), 0.0).then_inc(s_init, 1)
                pool.memset(c.d[:, :, :, W + 1:W + 2].bitcast(f32), 0.0).then_inc(s_init, 1)
            pool_cycle(pool, -1, False, True, True)
            pool_cycle(pool, 0, True, True, True)
            with pool.Fori(1, B - 2) as i:
                pool_cycle(pool, i, True, True, True)
            pool_cycle(pool, B - 2, True, True, False)
            pool_cycle(pool, B - 1, True, False, False)

        @block.scalar
        def _(act):
            act_sqrt(act, cA.s_ve, cA.s_sd, col(cA, SD), col(cA, VE), 0)
            for g in range(NG):
                high_parts(act, cA, 0, g)
            act_cycle(act, -1, False, True, True)
            act_cycle(act, 0, True, True, True)
            with act.Fori(1, B - 2) as i:
                act_cycle(act, i, True, True, True)
            act_cycle(act, B - 2, True, True, False)
            act_cycle(act, B - 1, True, False, False)

        @block.vector
        def _(dve):
            for c in (cA, cD):
                dve.memset(c.win[:, 0, :], 0.0)
                ins = dve.memset(c.win[:, NBLK - 1, :], 0.0)
                if c is cA:
                    ins.then_inc(s_zero, 1)
                else:
                    ins.then_inc(s_zero, 1)
            dve.wait_ge(s_cst, 16)
            dve.wait_ge(s_wld, 16 * n_wld)
            n = 0
            for c in (cA, cC, cD):
                base = c.base[:, :].rearrange("p (x r c) -> p x r c", x=TAPS, r=OUT_ROWS)
                tmp = c.scaled[:, :].rearrange("p (x r c) -> p x r c", x=TAPS, r=OUT_ROWS)
                for dy in range(TAPS):
                    dve.tensor_tensor(
                        base if dy == 0 else tmp,
                        c.compact[:, dy, :, :].unsqueeze(2).broadcast_to([128, TAPS, OUT_ROWS, C]),
                        tap_mask[:, dy, :].unsqueeze(1).unsqueeze(3).broadcast_to([128, TAPS, OUT_ROWS, C]),
                        ALU.mult).then_inc(s_toep, 1)
                    n += 1
                    dve.wait_ge(s_toep, n)
                    if dy:
                        dve.tensor_tensor(base, base, tmp, ALU.add).then_inc(s_toep, 1)
                        n += 1
                        dve.wait_ge(s_toep, n)
            win_stats_1(dve, cA, 0)
            win_stats_2(dve, cA, 0)
            win_stats_3(dve, cA, 0)
            for g in range(NG):
                low_parts(dve, cA, 0, g)
            dve_cycle(dve, -1, False, True, True)
            dve_cycle(dve, 0, True, True, True)
            with dve.Fori(1, B - 2) as i:
                dve_cycle(dve, i, True, True, True)
            dve_cycle(dve, B - 2, True, True, False)
            dve_cycle(dve, B - 1, True, False, False)

        @block.tensor
        def _(pe):
            pe.wait_ge(s_cst, 16)
            pe.wait_ge(s_init, 7)
            win_mean(pe, cA, 0)
            win_var(pe, cA, 0)
            pe_cycle(pe, -1, False, True, True, None, None)
            pe_cycle(pe, 0, True, True, True, (cA, 0), (cA, 1))
            with pe.Fori(1, B - 2) as i:
                pe_cycle(pe, i, True, True, True, (cD, i - 1), (cA, i + 1))
            pe_cycle(pe, B - 2, True, True, False, (cD, B - 3), (cA, B - 1))
            pe_cycle(pe, B - 1, True, False, False, None, (cD, B - 2))


def kernel(x, L0_conv_weights, L0_conv_biases, L2_conv_weight, L3_conv_K):
    import concourse.bacc as bacc
    from concourse.bass_utils import run_bass_kernel_spmd

    def taps(w):
        return np.ascontiguousarray(w)

    arrays = {
        "x": np.ascontiguousarray(x),
        "w0": taps(np.transpose(np.asarray(L0_conv_weights), (1, 2, 3, 0))),
        "b0": np.ascontiguousarray(L0_conv_biases),
        "w2": taps(np.transpose(np.asarray(L2_conv_weight)[:, :, ::-1, ::-1], (1, 2, 3, 0))),
        "w3": taps(np.asarray(L3_conv_K).reshape(C, TAPS, TAPS, C)),
        "consts": shape_constants(),
    }
    nc = bacc.Bacc("TRN2", target_bir_lowering=False, num_devices=1)
    args = [nc.dram_tensor(n, a.shape, mybir.dt.from_np(a.dtype), kind="ExternalInput").ap()
            for n, a in arrays.items()]
    y = nc.dram_tensor("y", (B, C, H, W), mybir.dt.float32, kind="ExternalOutput").ap()
    build(nc, *args, y)
    r = run_bass_kernel_spmd(nc, [arrays], core_ids=[0])
    return r.results[0]["y"]
```

```python
import concourse.bass as bass
import numpy as np
from concourse import mybir
from contextlib import ExitStack

B, C, H, W = 8, 16, 128, 128
G = 8
GC = C // G
EPS = 1e-5
TAPS = 3
WIN = 8
OUT_ROWS = WIN - TAPS + 1
NBLK = -(-H // OUT_ROWS)
LAST_ROW = H + 1 - WIN
OP = OUT_ROWS * C
FULL = (NBLK - 1) * OUT_ROWS
SPLIT_G = [(0, 4), (4, 4), (8, 4), (12, 4), (16, 4), (20, 2)]
NG = len(SPLIT_G)
WN = TAPS * OP
NMAT = 4
ROUNDS = C // (2 * NMAT)
NCHK = C // NMAT
STEPS = 5

K_IDENT = 0
K_SELM = K_IDENT + 128
K_SELL = K_SELM + 128
K_RES = K_SELL + 128
K_TAP = K_RES + WN
K_HOT = K_TAP + TAPS * OUT_ROWS
K_EDGE = K_HOT + G
K_ALL = K_EDGE + 4


def window_row(k):
    return OUT_ROWS * k - 1 if k < NBLK - 1 else LAST_ROW


def shape_constants():
    c = np.zeros((128, K_ALL), np.float32)
    q = np.arange(128)
    row, ch = q // C, q % C
    c[:, K_IDENT:K_IDENT + 128] = np.eye(128)
    same_group = (ch[:, None] // GC) == (ch[None, :] // GC)
    n = GC * H * W
    inner = (row >= 1) & (row <= OUT_ROWS)
    c[:, K_SELM:K_SELM + 128] = same_group * inner[:, None] * ((NBLK - 1) * W / n)
    only_last = inner & (LAST_ROW + row >= FULL)
    c[:, K_SELL:K_SELL + 128] = same_group * only_last[:, None] * (W / n)
    res = np.zeros((128, TAPS, OUT_ROWS, C), np.float32)
    for r in range(1, OUT_ROWS + 1):
        for k in range(C):
            res[r * C + k, 1, r - 1, k] = 1.0
    c[:, K_RES:K_RES + WN] = res.reshape(128, WN)
    tap = np.zeros((128, TAPS, OUT_ROWS), np.float32)
    for dy in range(TAPS):
        for r in range(OUT_ROWS):
            tap[(row == r + dy), dy, r] = 1.0
    c[:, K_TAP:K_TAP + TAPS * OUT_ROWS] = tap.reshape(128, -1)
    c[q, K_HOT + ch // GC] = 1.0
    c[:, K_EDGE + 0] = row != 0
    c[:, K_EDGE + 1] = row != WIN - 1
    c[:, K_EDGE + 2] = row == 0
    c[:, K_EDGE + 3] = row == WIN - 1
    return c


def at(per, b, n=0):
    return b * per + n


def wait(eng, sem, value):
    if isinstance(value, int) and value <= 0:
        return
    eng.wait_ge(sem, value)


def build(nc, x, w0, b0, w2, w3, consts, y):
    f32, f32r = mybir.dt.float32, mybir.dt.float32r
    ALU, ACT, AX = mybir.AluOpType, mybir.ActivationFunctionType, mybir.AxisListType
    ctx = ExitStack()
    with ctx:
        def sb(name, shape, dt=f32):
            return ctx.enter_context(nc.sbuf_tensor(name, shape, dt))

        def pb(name, shape):
            return ctx.enter_context(nc.psum_tensor(name, shape, f32))

        def sem(name):
            return ctx.enter_context(nc.semaphore(name))

        cst = sb("cst", [128, K_ALL])
        ident = cst[:, K_IDENT:K_IDENT + 128]
        sel_main = cst[:, K_SELM:K_SELM + 128]
        sel_last = cst[:, K_SELL:K_SELL + 128]
        residual = cst[:, K_RES:K_RES + WN]
        tap_mask = cst[:, K_TAP:K_TAP + TAPS * OUT_ROWS].rearrange("p (d r) -> p d r", d=TAPS)
        onehot = cst[:, K_HOT:K_HOT + G]
        edge_keep = cst[:, K_EDGE:K_EDGE + 2]
        edge_drop = cst[:, K_EDGE + 2:K_EDGE + 4]
        ones_mean = sb("ones_mean", [128, 128])
        ones_var = sb("ones_var", [128, 128])
        ones_all = sb("ones_all", [128, 128])

        s_cst = sem("s_cst")
        s_wld = sem("s_wld")
        s_init = sem("s_init")
        s_pads = sem("s_pads")
        s_zero = sem("s_zero")
        s_toep = sem("s_toep")

        class Conv:

            def __init__(self, name, weights):
                self.name = name
                self.weights = weights
                self.win = sb(f"win_{name}", [128, NBLK, W])
                self.d = sb(f"d_{name}", [128, 2, NBLK, W + 2], f32r)
                self.out = sb(f"out_{name}", [OP, NBLK, W])
                self.compact = sb(f"compact_{name}", [128, TAPS, TAPS, C])
                self.base = sb(f"base_{name}", [128, WN])
                self.scaled = sb(f"scaled_{name}", [128, WN])
                self.w = sb(f"w_{name}", [128, 2, WN], f32r)
                self.col = sb(f"col_{name}", [128, 16])
                self.mv = sb(f"mv_{name}", [128, 2, 2])
                self.bn = sb(f"bn_{name}", [128, NBLK // 3 + 1, 6])
                self.s_win = sem(f"win_{name}_loaded")
                self.s_stat = sem(f"stat_{name}_ready")
                self.s_sum = sem(f"sum_{name}_ready")
                self.s_ve = sem(f"var_{name}_ready")
                self.s_sd = sem(f"sqrt_{name}_ready")
                self.s_fix = sem(f"win_{name}_fixed")
                self.s_w = sem(f"w_{name}_ready")
                self.s_dh = sem(f"dh_{name}_ready")
                self.s_dl = sem(f"dl_{name}_ready")
                self.s_acc = sem(f"acc_{name}_ready")
                self.s_out = sem(f"out_{name}_ready")
                self.s_chain = sem(f"chain_{name}")
                self.s_sent = sem(f"out_{name}_sent")

        cA, cC, cD = Conv("A", w0), Conv("C", w2), Conv("D", w3)
        s_pad = sem("pad_C_ready")
        bias = sb("bias", [OP, 1])

        x1 = sb("x1", [H, C, W])
        x2 = sb("x2", [H, C, W])
        DN = sb("DN", [H, C, W])
        st = sb("st", [128, G, 6])
        dev = sb("dev", [128, 2, G * 2])
        tB = sb("tB", [128, 6, G])
        tC = sb("tC", [128, 6, G])
        pick = sb("pick", [128, 2, G])
        R = [[sb(f"R{s}{j}", [128, NMAT, 128]) for j in range(2)] for s in range(2)]
        V = [sb(f"V{ch}", [128, NMAT, 128]) for ch in range(NCHK)]
        U = [sb(f"U{ch}", [128, NMAT, 128]) for ch in range(NCHK)]
        sums = sb("sums", [128, 2, C])
        top = sb("top", [2 * C, 1])
        diag = sb("diag", [2 * C, 2 * C])
        norms = sb("norms", [128, 2, C])
        scl = sb("scl", [128, 4, C])

        conv_ps = [pb(f"conv_ps{i}", [128, 4, W]) for i in range(2)]
        R_ps = [pb(f"R_ps{s}", [128, NMAT, 128]) for s in range(2)]
        V_ps = [pb(f"V_ps{s}", [128, NMAT, 128]) for s in range(2)]
        win_ps = pb("win_ps", [128, 512])
        row_ps = pb("row_ps", [128, 512])

        s_x1 = sem("x1_rows_loaded")
        sB_bn, sB_sum, sB_ve, sB_sd, sB_ready = (sem(f"rows_B_{n}") for n in ("stat", "sum", "var", "sqrt", "ready"))
        sC_bn, sC_sum, sC_ve, sC_sd, sC_ready = (sem(f"rows_C_{n}") for n in ("stat", "sum", "var", "sqrt", "ready"))
        s_chainB = sem("chain_B")
        s_chainC = sem("chain_rows_C")
        s_DN = sem("DN_ready")
        s_T = sem("transposed")
        s_Gr = sem("gram_ready")
        s_V0 = sem("V0_ready")
        s_abs = sem("abs_sums_ready")
        s_nT = sem("norms_transposed")
        s_dg = sem("diag_ready")
        s_nB = sem("norms_spread")
        s_sc = sem("scales_ready")
        s_V0s = sem("V0_scaled")
        s_R0 = sem("R0_ready")
        s_Rp = sem("R_product")
        s_Vp = sem("V_product")
        s_R = sem("R_ready")
        s_V = sem("V_ready")
        s_U = sem("U_ready")
        s_x2 = sem("x2_ready")
        s_ycol = sem("y_column_ready")
        s_y = sem("y_stored")

        block = ctx.enter_context(nc.Block())

        n_x = NBLK
        n_x1 = NBLK
        n_x2 = NBLK + 2
        n_x3 = 5
        n_y = NBLK + 1

        def load_x(eng, b):
            wait(eng, cA.s_dl, at(NG, b))
            for k in range(NBLK):
                h0 = window_row(k)
                lo, hi = max(h0, 0), min(h0 + WIN, H)
                eng.dma_start(cA.win[(lo - h0) * C:(hi - h0) * C, k, :],
                              x[bass.ds(b, 1), :, lo:hi, :].rearrange("b c h w -> (b h) c w"))\
                    .then_inc(cA.s_win, 16)

        def rows_from_windows(eng, b, g):
            if g == 0:
                wait(eng, s_x2, at(NCHK, b))
            eng.wait_ge(cA.s_out, at(NG, b, g + 1))
            k0, kn = SPLIT_G[g]
            for k in range(k0, k0 + kn):
                if k < NBLK - 1:
                    eng.dma_start(x1[OUT_ROWS * k:OUT_ROWS * (k + 1), :, :], cA.out[:, k, :])\
                        .then_inc(s_x1, 16)
                else:
                    first = FULL - (LAST_ROW + 1)
                    eng.dma_start(x1[FULL:H, :, :], cA.out[first * C:OP, k, :]).then_inc(s_x1, 16)

        def windows_from_rows(sp, b):
            wait(sp, cC.s_dl, at(NG, b))
            sp.wait_ge(s_x2, at(NCHK, b, NCHK))
            for k in range(NBLK):
                h0 = window_row(k)
                lo, hi = max(h0, 0), min(h0 + WIN, H)
                sp.dma_start(cC.win[(lo - h0) * C:(hi - h0) * C, k, :], x2[lo:hi, :, :])\
                    .then_inc(cC.s_win, 16)
            sp.dma_start(cC.win[0:C, 0, :], x2[H - 1:H, :, :]).then_inc(cC.s_win, 16)
            sp.dma_start(cC.win[(WIN - 1) * C:, NBLK - 1, :], x2[0:1, :, :]).then_inc(cC.s_win, 16)

        def windows_from_windows(sp, b):
            sp.wait_ge(cC.s_out, at(NG, b, NG))
            wait(sp, cD.s_dl, at(NG, b))
            o, w, last = cC.out, cD.win, NBLK - 1
            above = window_row(last) - OUT_ROWS * (last - 1)
            below = OUT_ROWS * last - (LAST_ROW + 1)
            sp.dma_start(w[C:C + OP, :, :], o[:, :, :]).then_inc(cD.s_win, 16)
            sp.dma_start(w[0:C, 1:last, :], o[OP - C:OP, 0:last - 1, :]).then_inc(cD.s_win, 16)
            sp.dma_start(w[0:C, last, :], o[above * C:(above + 1) * C, last - 1, :]).then_inc(cD.s_win, 16)
            sp.dma_start(w[(WIN - 1) * C:, 0:last - 1, :], o[0:C, 1:last, :]).then_inc(cD.s_win, 16)
            sp.dma_start(w[(WIN - 1) * C:, last - 1, :], o[below * C:(below + 1) * C, last, :])\
                .then_inc(cD.s_win, 16)

        def store_y(sp, b):
            def rows(lo, hi):
                return y[bass.ds(b, 1), :, lo:hi, :].rearrange("b c h w -> (b h) c w")
            wait(sp, s_ycol, at(1, b, 1))
            sp.dma_start(rows(H - 1, H), cC.out[OP - C:OP, NBLK - 1, :]).then_inc(s_y, 16)
            for g, (k0, kn) in enumerate(SPLIT_G):
                wait(sp, cD.s_out, at(NG, b, g + 1))
                for k in reversed(range(k0, k0 + kn)):
                    if k < NBLK - 1:
                        sp.dma_start(rows(OUT_ROWS * k, OUT_ROWS * (k + 1)), cD.out[:, k, :]).then_inc(s_y, 16)
                    else:
                        first = FULL - (LAST_ROW + 1)
                        sp.dma_start(rows(FULL, H - 1), cD.out[first * C:OP - C, k, :]).then_inc(s_y, 16)

        def newton(dve, link, inv, ve, sd, t1, t2):
            link(dve.reciprocal(t1, sd))
            link(dve.tensor_tensor(t2, t1, t1, ALU.mult))
            link(dve.tensor_tensor(t2, t2, ve, ALU.mult))
            link(dve.tensor_scalar(t2, t2, -0.5, 1.5, ALU.mult, ALU.add))
            link(dve.tensor_tensor(inv, t1, t2, ALU.mult))

        class Chain:

            def __init__(self, eng, s, per, b, done=0):
                self.eng, self.s, self.per, self.b, self.n = eng, s, per, b, done

            def __call__(self, ins):
                self.n += 1
                ins.then_inc(self.s, 1)
                self.eng.wait_ge(self.s, at(self.per, self.b, self.n))

        MEAN, NEG, VE, SD, T1, T2, INV, OUTB, DEV, ADD, SPARE = 0, 1, 2, 3, 4, 5, 6, 7, 8, 10, 12

        def col(c, j, n=1, rows=128):
            return c.col[0:rows, j:j + n]

        NWIN = 1 + 6 + 5 + 2

        def win_stats_1(dve, c, b):
            link = Chain(dve, c.s_chain, NWIN, b)
            dve.wait_ge(c.s_win, at(16 * (n_x if c is cA else n_x3), b, 16 * (n_x if c is cA else n_x3)))
            for j in range(NBLK // 3):
                dve.bn_stats(c.bn[:, j, :], c.win[:, 3 * j:3 * j + 3, :])
            link(dve.bn_stats(c.bn[:, NBLK // 3, :], c.win[:, NBLK - 1, :]))
            dve.memset(col(c, SPARE), 0.0)
            dve.bn_aggr(c.mv[:, 0, :], c.bn[:, 0:NBLK // 3, :])
            dve.bn_aggr(c.mv[:, 1, :], c.bn[:, NBLK // 3, :]).then_inc(c.s_stat, 1)
            return link

        def win_stats_2(dve, c, b):
            link = Chain(dve, c.s_chain, NWIN, b, 1)
            dve.wait_ge(c.s_sum, at(2, b, 1))
            link(dve.tensor_copy(col(c, MEAN), win_ps[:, 0:1]))
            link(dve.tensor_scalar(col(c, DEV, 2), c.mv[:, :, 0], col(c, MEAN), None, ALU.subtract))
            link(dve.tensor_tensor(col(c, DEV, 2), col(c, DEV, 2), col(c, DEV, 2), ALU.mult))
            dve.tensor_tensor(col(c, DEV, 2), col(c, DEV, 2), c.mv[:, :, 1], ALU.add).then_inc(c.s_stat, 1)
            link(dve.tensor_scalar(col(c, ADD, 2), edge_drop, col(c, MEAN), None, ALU.mult))
            link(dve.tensor_scalar(col(c, NEG), col(c, MEAN), -1.0, None, ALU.mult))
            dve.tensor_scalar(c.win[:, 0, :], c.win[:, 0, :], edge_keep[:, 0:1], col(c, ADD),
                              ALU.mult, ALU.add)
            if c is cA:
                link(dve.tensor_tensor(col(c, OUTB, rows=OP), col(c, MEAN, rows=OP), bias[:, :], ALU.add))
            else:
                link(dve.tensor_copy(col(c, OUTB), col(c, MEAN)))
            dve.tensor_scalar(c.win[:, NBLK - 1, :], c.win[:, NBLK - 1, :], edge_keep[:, 1:2],
                              col(c, ADD + 1), ALU.mult, ALU.add).then_inc(c.s_fix, 1)

        def win_stats_3(dve, c, b):
            link = Chain(dve, c.s_chain, NWIN, b, 7)
            dve.wait_ge(c.s_sum, at(2, b, 2))
            dve.tensor_scalar(col(c, VE), win_ps[:, 1:2], EPS, None, ALU.add).then_inc(c.s_ve, 1)
            dve.wait_ge(c.s_sd, at(1, b, 1))
            newton(dve, link, col(c, INV), col(c, VE), col(c, SD), col(c, T1), col(c, T2))
            conv_weights(dve, link, c, b, col(c, INV))

        def conv_weights(dve, link, c, b, inv):
            wait(dve, c.s_acc, at(NG, b))
            link(dve.scalar_tensor_tensor(c.scaled[:, :], c.base[:, :], inv, residual, ALU.mult, ALU.add))
            link(dve.tensor_copy(c.w[:, 0, :], c.scaled[:, :]))
            dve.tensor_tensor(c.w[:, 1, :], c.scaled[:, :], c.w[:, 0, :].bitcast(f32), ALU.subtract)\
                .then_inc(c.s_w, 1)

        def low_parts(dve, c, b, g):
            k0, kn = SPLIT_G[g]
            dve.wait_ge(c.s_dh, at(NG, b, g + 1))
            dve.scalar_tensor_tensor(c.d[:, 1, k0:k0 + kn, 1:W + 1], c.win[:, k0:k0 + kn, :], col(c, MEAN),
                                     c.d[:, 0, k0:k0 + kn, 1:W + 1].bitcast(f32),
                                     ALU.subtract, ALU.subtract).then_inc(c.s_dl, 1)

        def high_parts(act, c, b, g):
            k0, kn = SPLIT_G[g]
            if g == 0:
                act.wait_ge(c.s_fix, at(1, b, 1))
                wait(act, c.s_acc, at(NG, b))
                if c is cC:
                    act.wait_ge(c.s_win, at(16 * n_x2, b, 16 * n_x2))
            act.activation(c.d[:, 0, k0:k0 + kn, 1:W + 1], c.win[:, k0:k0 + kn, :], ACT.Identity,
                           bias=col(c, NEG)).then_inc(c.s_dh, 1)

        def win_mean(pe, c, b):
            pe.wait_ge(c.s_stat, at(2, b, 1))
            pe.matmul(win_ps[:, 0:1], sel_main, c.mv[:, 0, 0:1], start=True, stop=False)
            pe.matmul(win_ps[:, 0:1], sel_last, c.mv[:, 1, 0:1], start=False, stop=True).then_inc(c.s_sum, 1)

        def win_var(pe, c, b):
            pe.wait_ge(c.s_stat, at(2, b, 2))
            pe.matmul(win_ps[:, 1:2], sel_main, col(c, DEV), start=True, stop=False)
            pe.matmul(win_ps[:, 1:2], sel_last, col(c, DEV + 1), start=False, stop=True).then_inc(c.s_sum, 1)

        NROW = 4 + 5

        def row_stats(dve, rows, s_bn, s_sum, s_ve, s_sd, chain, per, t, b):
            link = Chain(dve, chain, per, b)
            mean, inv, ve, sd, t1, t2 = (t[:, j, :] for j in range(6))
            for g in range(G):
                ins = dve.bn_stats(st[:, g, :], rows[:, GC * g:GC * (g + 1), :])
            ins.then_inc(s_bn, 1)
            halves = st[:, :, :].rearrange("p g (a t) -> p (g a) t", t=3)
            dve.wait_ge(s_bn, at(2, b, 1))
            dve.wait_ge(s_sum, at(2, b, 1))
            link(dve.tensor_reduce(mean, row_ps[:, 0:2 * G].rearrange("p (g a) -> p g a", a=2), AX.X, ALU.add))
            d, sq = dev[:, 0, :], dev[:, 1, :]
            link(dve.tensor_tensor(d.rearrange("p (g a) -> p g a", a=2),
                                   halves[:, :, 1].rearrange("p (g a) -> p g a", a=2),
                                   mean.unsqueeze(2).broadcast_to([128, G, 2]), ALU.subtract))
            link(dve.scalar_tensor_tensor(sq, d, float(GC * W // 2), d, ALU.mult, ALU.mult))
            dve.tensor_tensor(sq, sq, halves[:, :, 2], ALU.add).then_inc(s_bn, 1)
            dve.wait_ge(s_sum, at(2, b, 2))
            link(dve.tensor_reduce(t1, row_ps[:, 2 * G:4 * G].rearrange("p (g a) -> p g a", a=2), AX.X, ALU.add))
            dve.tensor_scalar(ve, t1, EPS, None, ALU.add).then_inc(s_ve, 1)
            dve.wait_ge(s_sd, at(1, b, 1))
            newton(dve, link, inv, ve, sd, t1, t2)
            return link

        def row_mean(pe, s_bn, s_sum, b):
            pe.wait_ge(s_bn, at(2, b, 1))
            pe.matmul(row_ps[:, 0:2 * G], ones_mean[:, :],
                      st[:, :, :].rearrange("p g (a t) -> p (g a) t", t=3)[:, :, 1],
                      start=True, stop=True).then_inc(s_sum, 1)

        def row_var(pe, s_bn, s_sum, b):
            pe.wait_ge(s_bn, at(2, b, 2))
            pe.matmul(row_ps[:, 2 * G:4 * G], ones_var[:, :], dev[:, 1, :], start=True, stop=True)\
                .then_inc(s_sum, 1)

        NG_EARLY = 4

        def conv_group(pe, c, b, g, prev, beside=False):
            k0, kn = SPLIT_G[g]
            if g == 0:
                pe.wait_ge(c.s_w, at(1, b, 1))
            pe.wait_ge(c.s_dl, at(NG, b, g + 1))
            if c is cC:
                pe.wait_ge(s_pad, at(NG, b, g + 1))
            if c is cC and g >= NG_EARLY and beside:
                pe.wait_ge(s_V0, at(NCHK, b + 1, 2 + g % 2 + 1))
            elif g >= 2:
                pe.wait_ge(c.s_out, at(NG, b, g - 1))
            elif prev is not None:
                pe.wait_ge(prev[0].s_out, at(NG, prev[1], NG - 1 + g))
            n = 0
            for dx in range(TAPS):
                for wp, dp in ((0, 0), (0, 1), (1, 0)):
                    ins = pe.matmul(conv_ps[g % 2][0:OP, 0:kn, :], c.w[:, wp, dx * OP:(dx + 1) * OP],
                                    c.d[:, dp, k0:k0 + kn, dx:dx + W], start=n == 0, stop=n == 8)
                    n += 1
            ins.then_inc(c.s_acc, 1)

        def conv_out(act, c, b, g):
            k0, kn = SPLIT_G[g]
            act.wait_ge(c.s_acc, at(NG, b, g + 1))
            if g == 0:
                if c is cA:
                    wait(act, s_x1, at(16 * n_x1, b))
                if c is cC:
                    wait(act, cD.s_win, at(16 * n_x3, b))
                    wait(act, s_ycol, at(1, b))
                if c is cC or c is cD:
                    wait(act, s_y, at(16 * n_y, b))
            wn = W - 1 if c is cD else W
            act.activation(c.out[:, k0:k0 + kn, 0:wn], conv_ps[g % 2][0:OP, 0:kn, 0:wn], ACT.Identity,
                           bias=col(c, OUTB, rows=OP)).then_inc(c.s_out, 1)

        def copy_column(pool, out, in_):
            p, *n = out.shape
            ones = ones_all[0:p, 0:int(np.prod(n))]
            if len(n) == 3:
                ones = ones.rearrange("p (a k o) -> p a k o", a=n[0], o=1)
            else:
                ones = ones.unsqueeze(2)
            return pool.tensor_tensor(out, in_, ones, ALU.mult)

        def y_column(pool, i):
            pool.wait_ge(cC.s_out, at(NG, i, NG))
            wait(pool, s_y, at(16 * n_y, i))
            copy_column(pool, cD.out[:, :, W - 1:W], cC.out[:, :, W - 1:W]).then_inc(s_ycol, 1)

        per_R = NCHK * (STEPS - 1)
        per_V = NCHK * (STEPS - 1)
        per_Vp = NCHK * STEPS
        T_ps = [V_ps[0], V_ps[1], conv_ps[0], conv_ps[1]]

        def n_R(r, k, s):
            return 2 * (STEPS - 1) * r + 2 * k + s + 1

        def n_Vp(r, k, s):
            return 2 * STEPS * r + 2 * k + s + 1

        def sp_cycle(sp, i, prev, nxt, nxt2):
            if prev:
                windows_from_windows(sp, i - 1)
            windows_from_rows(sp, i)
            if prev:
                store_y(sp, i - 1)

        def pe_gram(pe, b, ch):
            s = ch % 2
            if ch >= 2:
                pe.wait_ge(s_R, at(per_R, b, n_R(0, STEPS - 2, s)))
            for m in range(NMAT):
                ins = pe.matmul(R_ps[s][:, m, :], DN[:, NMAT * ch + m, :], DN[:, NMAT * ch + m, :],
                                start=True, stop=True)
            ins.then_inc(s_Gr, 1)

        def pe_norms(pe, b, prev):
            if prev:
                for g in range(NG_EARLY):
                    conv_group(pe, cC, b - 1, g, (cD, b - 2) if not isinstance(b, int) or b >= 2 else (cA, b))
            wait(pe, s_x2, at(NCHK, b))
            for ch in range(NCHK):
                pe.wait_ge(s_DN, at(NCHK, b, ch + 1))
                if ch >= 2:
                    if prev:
                        pe.wait_ge(cC.s_out, at(NG, b - 1, NG_EARLY - 2 + ch - 1))
                    else:
                        pe.wait_ge(cA.s_out, at(NG, b, NG))
                for m in range(NMAT):
                    ins = pe.transpose(T_ps[ch][:, m, :], DN[:, NMAT * ch + m, :], ident)
                ins.then_inc(s_T, 1)
            pe_gram(pe, b, 0)
            pe_gram(pe, b, 1)
            if prev:
                conv_group(pe, cC, b - 1, NG_EARLY, None, True)
            pe.wait_ge(s_abs, at(1, b, 1))
            pe.transpose(row_ps[0:2 * C, 128:256], sums[:, :, :].rearrange("p a c -> p (a c)"), ident)\
                .then_inc(s_nT, 1)
            if prev:
                conv_group(pe, cC, b - 1, NG_EARLY + 1, None, True)
            pe.wait_ge(s_dg, at(1, b, 1))
            pe.matmul(row_ps[:, 256:256 + 2 * C], ones_all[0:2 * C, :], diag[:, :], start=True, stop=True)\
                .then_inc(s_nB, 1)

        def pe_step(pe, b, r, k):
            for s in range(2):
                ch = 2 * r + s
                Rk = R[s][(k + r) % 2]
                if k == 0:
                    pe.wait_ge(s_R0, at(NCHK, b, ch + 1))
                    pe.wait_ge(s_V0, at(NCHK, b, ch + 1))
                    if r > 0:
                        pe.wait_ge(s_x2, at(NCHK, b, ch - 1))
                else:
                    pe.wait_ge(s_R, at(per_R, b, n_R(r, k - 1, s)))
                if k < STEPS - 1:
                    for m in range(NMAT):
                        ins = pe.matmul(R_ps[s][:, m, :], Rk[:, m, :], Rk[:, m, :], start=True, stop=True)
                    ins.then_inc(s_Rp, 1)
                elif r + 1 < ROUNDS:
                    pe_gram(pe, b, ch + 2)
                if k > 0:
                    pe.wait_ge(s_V, at(per_V, b, n_R(r, k - 1, s)))
                for m in range(NMAT):
                    ins = pe.matmul(V_ps[s][:, m, :], Rk[:, m, :], V[ch][:, m, :], start=True, stop=True)
                ins.then_inc(s_Vp, 1)

        def pe_cycle(pe, i, prev, nxt, nxt2):
            pe_norms(pe, i, prev)
            if nxt:
                win_mean(pe, cA, i + 1)
            for k in range(STEPS):
                pe_step(pe, i, 0, k)
                if nxt and k == 0:
                    win_var(pe, cA, i + 1)
                if prev and k == 3:
                    win_mean(pe, cD, i - 1)
            for k in range(STEPS):
                pe_step(pe, i, 1, k)
                if prev and k == 0:
                    win_var(pe, cD, i - 1)
            before = (cC, i - 1) if prev else (cA, i)
            for g in range(NG):
                if nxt:
                    conv_group(pe, cA, i + 1, g, before)
                if g == 1:
                    row_mean(pe, sC_bn, sC_sum, i)
                if g == 2:
                    row_var(pe, sC_bn, sC_sum, i)
            if nxt:
                before = (cA, i + 1)
            for g in range(NG):
                if prev:
                    conv_group(pe, cD, i - 1, g, before)
                if nxt and g == 3:
                    row_mean(pe, sB_bn, sB_sum, i + 1)
                if nxt and g == 4:
                    row_var(pe, sB_bn, sB_sum, i + 1)

        def pe_end(pe):
            i = B - 1
            for g in range(NG):
                conv_group(pe, cC, i, g, (cD, i - 1))
            win_mean(pe, cD, i)
            win_var(pe, cD, i)
            for g in range(NG):
                conv_group(pe, cD, i, g, (cC, i))

        def act_sqrt(act, s_ve, s_sd, out, in_, b):
            act.wait_ge(s_ve, at(1, b, 1))
            act.activation(out, in_, ACT.Sqrt).then_inc(s_sd, 1)

        def act_norms(act, b, prev):
            if prev:
                for g in range(NG_EARLY):
                    conv_out(act, cC, b - 1, g)
            for ch in (0, 1, 2, 3):
                act.wait_ge(s_T, at(NCHK, b, ch + 1))
                act.activation(V[ch][:, :, :], T_ps[ch][:, :, :], ACT.Copy).then_inc(s_V0, 1)
            if prev:
                for g in range(NG_EARLY, NG):
                    conv_out(act, cC, b - 1, g)

        def act_step(act, b, r, k):
            for s in range(2):
                act.wait_ge(s_Rp, at(per_R, b, n_R(r, k, s)))
                if k > 0:
                    act.wait_ge(s_Vp, at(per_Vp, b, n_Vp(r, k - 1, s)))
                act.activation(R[s][(k + 1 + r) % 2][:, :, :], R_ps[s][:, :, :], ACT.Copy).then_inc(s_R, 1)

        def win_sqrt(act, c, b):
            act_sqrt(act, c.s_ve, c.s_sd, col(c, SD), col(c, VE), b)

        def act_cycle(act, i, prev, nxt, nxt2):
            act_norms(act, i, prev)
            for k in range(STEPS - 1):
                act_step(act, i, 0, k)
                if nxt:
                    if k == 0:
                        win_sqrt(act, cA, i + 1)
                    if k >= 1:
                        high_parts(act, cA, i + 1, k - 1)
            for k in range(STEPS - 1):
                act_step(act, i, 1, k)
                if prev and k == 0:
                    win_sqrt(act, cD, i - 1)
                if nxt and k >= 1:
                    high_parts(act, cA, i + 1, k + 2)
            if not nxt:
                act_sqrt(act, sC_ve, sC_sd, tC[:, 3, :], tC[:, 2, :], i)
            for g in range(NG):
                if prev:
                    high_parts(act, cD, i - 1, g)
                if nxt:
                    conv_out(act, cA, i + 1, g)
                    if g > 0:
                        rows_from_windows(act, i + 1, g - 1)
                    if g == 2:
                        act_sqrt(act, sC_ve, sC_sd, tC[:, 3, :], tC[:, 2, :], i)
            if nxt:
                rows_from_windows(act, i + 1, NG - 1)
            for g in range(NG):
                if prev:
                    conv_out(act, cD, i - 1, g)
                if g == 2:
                    high_parts(act, cC, i, 0)
                if g == 3:
                    high_parts(act, cC, i, 1)
                    high_parts(act, cC, i, 2)
                if g == 4:
                    if nxt:
                        act_sqrt(act, sB_ve, sB_sd, tB[:, 3, :], tB[:, 2, :], i + 1)
                    high_parts(act, cC, i, 3)
            high_parts(act, cC, i, 4)
            high_parts(act, cC, i, 5)

        def act_end(act):
            i = B - 1
            for g in range(NG):
                conv_out(act, cC, i, g)
            win_sqrt(act, cD, i)
            for g in range(NG):
                high_parts(act, cD, i, g)
            for g in range(NG):
                conv_out(act, cD, i, g)

        NROW_B = NROW + 1
        perB = NROW_B + 6
        perRC = NROW + 4 + 2

        def dve_norms(dve, b):
            link = Chain(dve, s_chainB, perB, b, NROW_B)
            for ch in range(NCHK):
                dve.wait_ge(s_DN, at(NCHK, b, ch + 1))
                dve.tensor_reduce(sums[:, 0, NMAT * ch:NMAT * (ch + 1)], DN[:, NMAT * ch:NMAT * (ch + 1), :],
                                  AX.X, ALU.add, apply_absolute_value=True)
            for ch in range(NCHK):
                dve.wait_ge(s_V0, at(NCHK, b, ch + 1))
                ins = dve.tensor_reduce(sums[:, 1, NMAT * ch:NMAT * (ch + 1)], V[ch][:, :, :],
                                        AX.X, ALU.add, apply_absolute_value=True)
            ins.then_inc(s_abs, 1)
            dve.wait_ge(s_nT, at(1, b, 1))
            link(dve.tensor_reduce(top[:, :], row_ps[0:2 * C, 128:256], AX.X, ALU.max))
            dve.tensor_scalar(diag[:, :], ident[0:2 * C, 0:2 * C], top[:, :], None, ALU.mult)\
                .then_inc(s_dg, 1)
            dve.wait_ge(s_nB, at(1, b, 1))
            link(dve.tensor_copy(norms[:, :, :].rearrange("p a c -> p (a c)"), row_ps[:, 256:256 + 2 * C]))
            link(dve.tensor_tensor(scl[:, 0, :], norms[:, 0, :], norms[:, 1, :], ALU.mult))
            link(dve.reciprocal(scl[:, 1, :], scl[:, 0, :]))
            link(dve.tensor_scalar(scl[:, 2, :], scl[:, 1, :], -1.0, None, ALU.mult))
            ins = dve.tensor_tensor(scl[:, 3, :].rearrange("p (g a) -> p g a", a=GC),
                                    scl[:, 1, :].rearrange("p (g a) -> p g a", a=GC),
                                    tB[:, 4, :].unsqueeze(2).broadcast_to([128, G, GC]), ALU.mult)
            link(ins)

        def dve_R0(dve, b, ch):
            s = ch % 2
            dve.wait_ge(s_Gr, at(NCHK, b, ch + 1))
            if ch >= 2:
                dve.wait_ge(s_Vp, at(per_Vp, b, n_Vp(0, STEPS - 2, s)))
            for m in range(NMAT):
                ins = dve.scalar_tensor_tensor(R[s][ch // 2][:, m, :], R_ps[s][:, m, :],
                                               scl[:, 2, NMAT * ch + m:NMAT * ch + m + 1], ident,
                                               ALU.mult, ALU.add)
            ins.then_inc(s_R0, 1)

        def dve_step(dve, b, r, k):
            for s in range(2):
                ch = 2 * r + s
                if k == STEPS - 1 and r + 1 < ROUNDS:
                    dve_R0(dve, b, ch + 2)
                dve.wait_ge(s_Vp, at(per_Vp, b, n_Vp(r, k, s)))
                if k == 0:
                    dve.wait_ge(s_V0s, at(NCHK, b, ch + 1))
                    for m in range(NMAT):
                        ins = dve.scalar_tensor_tensor(V[ch][:, m, :], V_ps[s][:, m, :],
                                                       scl[:, 3, NMAT * ch + m:NMAT * ch + m + 1],
                                                       U[ch][:, m, :], ALU.mult, ALU.add)
                    ins.then_inc(s_V, 1)
                elif k < STEPS - 1:
                    dve.wait_ge(s_V, at(per_V, b, n_R(r, k - 1, s)))
                    dve.tensor_tensor(V[ch][:, :, :], V_ps[s][:, :, :], V[ch][:, :, :], ALU.add)\
                        .then_inc(s_V, 1)
                else:
                    dve.wait_ge(s_U, at(NCHK, b, ch + 1))
                    if ch == 0:
                        wait(dve, cC.s_win, at(16 * n_x2, b))
                    dve.tensor_tensor(x2[:, NMAT * ch:NMAT * (ch + 1), :], V_ps[s][:, :, :],
                                      U[ch][:, :, :], ALU.add).then_inc(s_x2, 1)

        def dve_rows_B(dve, b):
            dve.wait_ge(s_x1, at(16 * n_x1, b, 16 * n_x1))
            link = row_stats(dve, x1, sB_bn, sB_sum, sB_ve, sB_sd, s_chainB, perB, tB, b)
            link(dve.tensor_tensor(tB[:, 4, :], tB[:, 2, :], tB[:, 1, :], ALU.mult))
            assert link.n == NROW_B, link.n

        def dve_rows_C(dve, b):
            dve.wait_ge(s_x2, at(NCHK, b, NCHK))
            link = row_stats(dve, x2, sC_bn, sC_sum, sC_ve, sC_sd, s_chainC, perRC, tC, b)
            link(dve.tensor_tensor(pick[:, :, :], tC[:, 0:2, :],
                                   onehot.unsqueeze(1).broadcast_to([128, 2, G]), ALU.mult))
            link(dve.tensor_reduce(col(cC, MEAN), pick[:, 0, :], AX.X, ALU.add))
            link(dve.tensor_reduce(col(cC, INV), pick[:, 1, :], AX.X, ALU.add))
            link(dve.tensor_copy(col(cC, OUTB), col(cC, MEAN)))
            dve.tensor_scalar(col(cC, NEG), col(cC, MEAN), -1.0, None, ALU.mult).then_inc(cC.s_fix, 1)
            conv_weights(dve, link, cC, b, col(cC, INV))
            assert link.n == perRC, link.n

        def dve_cycle(dve, i, prev, nxt, nxt2):
            dve_norms(dve, i)
            dve_R0(dve, i, 0)
            dve_R0(dve, i, 1)
            if nxt:
                win_stats_2(dve, cA, i + 1)
            for k in range(STEPS):
                dve_step(dve, i, 0, k)
                if nxt and k == 0:
                    win_stats_3(dve, cA, i + 1)
                if prev and k == 2:
                    win_stats_1(dve, cD, i - 1)
                if nxt and k in (1, 3):
                    low_parts(dve, cA, i + 1, (k - 1) // 2)
            if prev:
                win_stats_2(dve, cD, i - 1)
            for k in range(STEPS):
                dve_step(dve, i, 1, k)
                if prev and k == 0:
                    win_stats_3(dve, cD, i - 1)
                if nxt and k >= 1:
                    low_parts(dve, cA, i + 1, k + 1)
            dve_rows_C(dve, i)
            if prev:
                for g in range(NG):
                    low_parts(dve, cD, i - 1, g)
            if nxt:
                dve_rows_B(dve, i + 1)
            for g in range(NG):
                low_parts(dve, cC, i, g)
            if nxt2:
                win_stats_1(dve, cA, i + 2)

        def dve_end(dve):
            win_stats_1(dve, cD, B - 1)
            win_stats_2(dve, cD, B - 1)
            win_stats_3(dve, cD, B - 1)
            for g in range(NG):
                low_parts(dve, cD, B - 1, g)

        def pool_DN(pool, b):
            pool.wait_ge(sB_bn, at(2, b, 2))
            wait(pool, s_x2, at(NCHK, b))
            for ch in range(NCHK):
                gs = slice(ch * NMAT // GC, (ch + 1) * NMAT // GC)
                pool.tensor_tensor(
                    DN[:, NMAT * ch:NMAT * (ch + 1), :].rearrange("p (g a) w -> p g (a w)", a=GC),
                    x1[:, NMAT * ch:NMAT * (ch + 1), :].rearrange("p (g a) w -> p g (a w)", a=GC),
                    tB[:, 0, gs].unsqueeze(2).broadcast_to([128, NMAT // GC, GC * W]),
                    ALU.subtract).then_inc(s_DN, 1)

        def pool_cycle(pool, i, prev, nxt, nxt2):
            for ch in range(NCHK):
                pool.wait_ge(s_R0, at(NCHK, i, 1))
                pool.tensor_tensor(U[ch][:, :, :], V[ch][:, :, :],
                                   scl[:, 3, NMAT * ch:NMAT * (ch + 1)].unsqueeze(2)
                                   .broadcast_to([128, NMAT, 128]), ALU.mult).then_inc(s_V0s, 1)
            if prev:
                y_column(pool, i - 1)
            for ch in range(NCHK):
                pool.wait_ge(s_V, at(per_V, i, n_R(ch // 2, STEPS - 2, ch % 2)))
                pool.tensor_tensor(U[ch][:, :, :], V[ch][:, :, :], x1[:, NMAT * ch:NMAT * (ch + 1), :],
                                   ALU.add).then_inc(s_U, 1)
            if nxt2:
                load_x(pool, i + 2)
            if nxt:
                pool_DN(pool, i + 1)
            for g, (k0, kn) in enumerate(SPLIT_G):
                pool.wait_ge(cC.s_dl, at(NG, i, g + 1))
                d = cC.d[:, :, k0:k0 + kn, :]
                copy_column(pool, d[:, :, :, 0:1], d[:, :, :, W:W + 1].bitcast(f32))
                copy_column(pool, d[:, :, :, W + 1:W + 2], d[:, :, :, 1:2].bitcast(f32)).then_inc(s_pad, 1)

        n_wld = 3 * WIN + OUT_ROWS

        def cycles(eng, cycle):
            cycle(eng, 0, False, True, True)
            cycle(eng, 1, True, True, True)
            with eng.Fori(2, B - 2) as i:
                cycle(eng, i, True, True, True)
            cycle(eng, B - 2, True, True, False)
            cycle(eng, B - 1, True, False, False)

        @block.sync
        def _(sp):
            sp.dma_start(cst[:, :], consts).then_inc(s_cst, 16)
            for j in range(OUT_ROWS):
                sp.dma_start(bias[j * C:(j + 1) * C, :], b0.rearrange("(c a) -> c a", a=1)).then_inc(s_wld, 16)
            for c in (cA, cC, cD):
                for j in range(WIN):
                    sp.dma_start(c.compact[j * C:(j + 1) * C, :, :, :], c.weights).then_inc(s_wld, 16)
            cycles(sp, sp_cycle)
            windows_from_windows(sp, B - 1)
            store_y(sp, B - 1)
            sp.wait_ge(s_y, 16 * n_y * B)

        @block.gpsimd
        def _(pool):
            pool.wait_ge(s_zero, 1)
            load_x(pool, 0)
            pool.memset(ones_mean[:, :], 1.0 / (GC * W)).then_inc(s_init, 1)
            pool.memset(ones_var[:, :], 1.0 / (GC * H * W)).then_inc(s_init, 1)
            pool.memset(ones_all[:, :], 1.0).then_inc(s_init, 1)
            for c in (cA, cD):
                pool.memset(c.d[:, :, :, 0:1].bitcast(f32), 0.0).then_inc(s_init, 1)
                pool.memset(c.d[:, :, :, W + 1:W + 2].bitcast(f32), 0.0).then_inc(s_init, 1)
            load_x(pool, 1)
            pool_DN(pool, 0)
            cycles(pool, pool_cycle)
            y_column(pool, B - 1)

        @block.scalar
        def _(act):
            win_sqrt(act, cA, 0)
            for g in range(NG):
                high_parts(act, cA, 0, g)
            for g in range(NG):
                conv_out(act, cA, 0, g)
                rows_from_windows(act, 0, g)
            act_sqrt(act, sB_ve, sB_sd, tB[:, 3, :], tB[:, 2, :], 0)
            cycles(act, act_cycle)
            act_end(act)

        @block.vector
        def _(dve):
            for c in (cA, cD):
                dve.memset(c.win[:, 0, :], 0.0)
                ins = dve.memset(c.win[:, NBLK - 1, :], 0.0)
                if c is cA:
                    ins.then_inc(s_zero, 1)
                else:
                    ins.then_inc(s_zero, 1)
            dve.wait_ge(s_cst, 16)
            dve.wait_ge(s_wld, 16 * n_wld)
            n = 0
            for c in (cA, cC, cD):
                base = c.base[:, :].rearrange("p (x r c) -> p x r c", x=TAPS, r=OUT_ROWS)
                tmp = c.scaled[:, :].rearrange("p (x r c) -> p x r c", x=TAPS, r=OUT_ROWS)
                for dy in range(TAPS):
                    dve.tensor_tensor(
                        base if dy == 0 else tmp,
                        c.compact[:, dy, :, :].unsqueeze(2).broadcast_to([128, TAPS, OUT_ROWS, C]),
                        tap_mask[:, dy, :].unsqueeze(1).unsqueeze(3).broadcast_to([128, TAPS, OUT_ROWS, C]),
                        ALU.mult).then_inc(s_toep, 1)
                    n += 1
                    dve.wait_ge(s_toep, n)
                    if dy:
                        dve.tensor_tensor(base, base, tmp, ALU.add).then_inc(s_toep, 1)
                        n += 1
                        dve.wait_ge(s_toep, n)
            win_stats_1(dve, cA, 0)
            win_stats_2(dve, cA, 0)
            win_stats_3(dve, cA, 0)
            for g in range(NG):
                low_parts(dve, cA, 0, g)
            dve_rows_B(dve, 0)
            win_stats_1(dve, cA, 1)
            cycles(dve, dve_cycle)
            dve_end(dve)

        @block.tensor
        def _(pe):
            pe.wait_ge(s_cst, 16)
            pe.wait_ge(s_init, 7)
            win_mean(pe, cA, 0)
            win_var(pe, cA, 0)
            for g in range(NG):
                conv_group(pe, cA, 0, g, None)
            row_mean(pe, sB_bn, sB_sum, 0)
            row_var(pe, sB_bn, sB_sum, 0)
            cycles(pe, pe_cycle)
            pe_end(pe)


def kernel(x, L0_conv_weights, L0_conv_biases, L2_conv_weight, L3_conv_K):
    import concourse.bacc as bacc
    from concourse.bass_utils import run_bass_kernel_spmd

    def taps(w):
        return np.ascontiguousarray(w)

    arrays = {
        "x": np.ascontiguousarray(x),
        "w0": taps(np.transpose(np.asarray(L0_conv_weights), (1, 2, 3, 0))),
        "b0": np.ascontiguousarray(L0_conv_biases),
        "w2": taps(np.transpose(np.asarray(L2_conv_weight)[:, :, ::-1, ::-1], (1, 2, 3, 0))),
        "w3": taps(np.asarray(L3_conv_K).reshape(C, TAPS, TAPS, C)),
        "consts": shape_constants(),
    }
    nc = bacc.Bacc("TRN2", target_bir_lowering=False, num_devices=1)
    args = [nc.dram_tensor(n, a.shape, mybir.dt.from_np(a.dtype), kind="ExternalInput").ap()
            for n, a in arrays.items()]
    y = nc.dram_tensor("y", (B, C, H, W), mybir.dt.float32, kind="ExternalOutput").ap()
    build(nc, *args, y)
    r = run_bass_kernel_spmd(nc, [arrays], core_ids=[0])
    return r.results[0]["y"]
```

```python
import concourse.bass as bass
import numpy as np
from concourse import mybir
from contextlib import ExitStack

B, C, H, W = 8, 16, 128, 128
G = 8
GC = C // G
EPS = 1e-5
TAPS = 3
WIN = 8
OUT_ROWS = WIN - TAPS + 1
NBLK = -(-H // OUT_ROWS)
LAST_ROW = H + 1 - WIN
OP = OUT_ROWS * C
FULL = (NBLK - 1) * OUT_ROWS
SPLIT_G = [(0, 4), (4, 4), (8, 4), (12, 4), (16, 4), (20, 2)]
NG = len(SPLIT_G)
WN = TAPS * OP
NMAT = 4
ROUNDS = C // (2 * NMAT)
NCHK = C // NMAT
STEPS = 5

K_IDENT = 0
K_SEL = K_IDENT + 128
K_RES = K_SEL + 128
K_TAP = K_RES + WN
K_HOT = K_TAP + TAPS * OUT_ROWS
K_EDGE = K_HOT + G
K_SHARE = K_EDGE + 4
K_ALL = K_SHARE + 4


def window_row(k):
    return OUT_ROWS * k - 1 if k < NBLK - 1 else LAST_ROW


def shape_constants():
    c = np.zeros((128, K_ALL), np.float32)
    q = np.arange(128)
    row, ch = q // C, q % C
    c[:, K_IDENT:K_IDENT + 128] = np.eye(128)
    same_group = (ch[:, None] // GC) == (ch[None, :] // GC)
    n = GC * H * W
    c[:, K_SEL:K_SEL + 128] = same_group
    inner = (row >= 1) & (row <= OUT_ROWS)
    c[:, K_SHARE + 0] = inner * ((NBLK - 1) * W / n)
    c[:, K_SHARE + 1] = (inner & (LAST_ROW + row >= FULL)) * (W / n)
    c[:, K_SHARE + 2] = (row < OUT_ROWS) * ((NBLK - 1) * W / n)
    c[:, K_SHARE + 3] = ((row < OUT_ROWS) & (LAST_ROW + 1 + row >= FULL)) * (W / n)
    res = np.zeros((128, TAPS, OUT_ROWS, C), np.float32)
    for r in range(1, OUT_ROWS + 1):
        for k in range(C):
            res[r * C + k, 1, r - 1, k] = 1.0
    c[:, K_RES:K_RES + WN] = res.reshape(128, WN)
    tap = np.zeros((128, TAPS, OUT_ROWS), np.float32)
    for dy in range(TAPS):
        for r in range(OUT_ROWS):
            tap[(row == r + dy), dy, r] = 1.0
    c[:, K_TAP:K_TAP + TAPS * OUT_ROWS] = tap.reshape(128, -1)
    c[q, K_HOT + ch // GC] = 1.0
    c[:, K_EDGE + 0] = row != 0
    c[:, K_EDGE + 1] = row != WIN - 1
    c[:, K_EDGE + 2] = row == 0
    c[:, K_EDGE + 3] = row == WIN - 1
    return c


def at(per, b, n=0):
    return b * per + n


def wait(eng, sem, value):
    if isinstance(value, int) and value <= 0:
        return
    eng.wait_ge(sem, value)


def build(nc, x, w0, b0, w2, w3, consts, y, rows_dram):
    f32, f32r = mybir.dt.float32, mybir.dt.float32r
    ALU, ACT, AX = mybir.AluOpType, mybir.ActivationFunctionType, mybir.AxisListType
    ctx = ExitStack()
    with ctx:
        def sb(name, shape, dt=f32):
            return ctx.enter_context(nc.sbuf_tensor(name, shape, dt))

        def pb(name, shape):
            return ctx.enter_context(nc.psum_tensor(name, shape, f32))

        def sem(name):
            return ctx.enter_context(nc.semaphore(name))

        cst = sb("cst", [128, K_ALL])
        ident = cst[:, K_IDENT:K_IDENT + 128]
        same_group = cst[:, K_SEL:K_SEL + 128]
        share = cst[:, K_SHARE:K_SHARE + 4]
        residual = cst[:, K_RES:K_RES + WN]
        tap_mask = cst[:, K_TAP:K_TAP + TAPS * OUT_ROWS].rearrange("p (d r) -> p d r", d=TAPS)
        onehot = cst[:, K_HOT:K_HOT + G]
        edge_keep = cst[:, K_EDGE:K_EDGE + 2]
        edge_drop = cst[:, K_EDGE + 2:K_EDGE + 4]
        ones_mean = sb("ones_mean", [128, 128])
        ones_var = sb("ones_var", [128, 128])
        ones_all = sb("ones_all", [128, 128])

        s_cst = sem("constants_loaded")
        s_wld = sem("taps_A_loaded")
        s_wrest = sem("taps_C_D_and_bias_loaded")
        s_init = sem("pool_memset_done")
        s_zero = sem("window_edges_zeroed")
        s_toep = sem("stationary_step_done")

        class Conv:

            def __init__(self, name, weights, d=None):
                self.name = name
                self.weights = weights
                self.win = sb(f"win_{name}", [128, NBLK, W])
                self.d = sb(f"d_{name}", [128, 2, NBLK, W + 2], f32r) if d is None else d
                self.out = sb(f"out_{name}", [OP, NBLK, W])
                self.compact = sb(f"compact_{name}", [128, TAPS, TAPS, C])
                self.base = sb(f"base_{name}", [128, WN])
                self.scaled = sb(f"scaled_{name}", [128, WN])
                self.w = sb(f"w_{name}", [128, 2, WN], f32r)
                self.col = sb(f"col_{name}", [128, 16])
                self.mv = sb(f"mv_{name}", [128, 2, 2])
                self.bn = sb(f"bn_{name}", [128, NBLK // 3 + 1, 6])
                self.s_win = sem(f"win_{name}_loaded")
                self.s_stat = sem(f"stat_{name}_ready")
                self.s_sum = sem(f"sum_{name}_ready")
                self.s_ve = sem(f"var_{name}_ready")
                self.s_sd = sem(f"sqrt_{name}_ready")
                self.s_fix = sem(f"win_{name}_fixed")
                self.s_w = sem(f"w_{name}_ready")
                self.s_dh = sem(f"dh_{name}_ready")
                self.s_dl = sem(f"dl_{name}_ready")
                self.s_acc = sem(f"acc_{name}_ready")
                self.s_out = sem(f"out_{name}_ready")
                self.s_chain = sem(f"chain_{name}")

        class Lodger:

            def __init__(self, name, own, host):
                self.name, self.base = name, own.base
                self.win, self.d, self.out, self.w, self.scaled = host.win, host.d, host.out, host.w, host.scaled
                self.col = sb(f"col_{name}", [128, 16])
                self.mv = sb(f"mv_{name}", [128, 2, 2])
                self.bn = sb(f"bn_{name}", [128, NBLK // 3 + 1, 6])
                self.s_stat, self.s_sum, self.s_ve, self.s_sd = own.s_stat, own.s_sum, own.s_ve, own.s_sd
                self.s_fix, self.s_w, self.s_dh, self.s_dl = own.s_fix, own.s_w, own.s_dh, own.s_dl
                self.s_acc, self.s_out, self.s_chain = own.s_acc, own.s_out, own.s_chain

        cA, cC = Conv("A", w0), Conv("C", w2)
        cD = Conv("D", w3, cA.d)
        cA1 = Lodger("A1", cA, cC)
        s_pad = sem("pad_C_ready")
        bias = sb("bias", [OP, 1])

        x1 = sb("x1", [H, C, W])
        x2 = sb("x2", [H, C, W])
        DN = sb("DN", [H, C, W])
        st = sb("st", [128, G, 6])
        dev = sb("dev", [128, 2, G * 2])
        tB = sb("tB", [128, 6, G])
        tC = sb("tC", [128, 6, G])
        pick = sb("pick", [128, 2, G])
        R = [[sb(f"R{s}{j}", [128, NMAT, 128]) for j in range(2)] for s in range(2)]
        V = [sb(f"V{ch}", [128, NMAT, 128]) for ch in range(NCHK)]
        U = [sb(f"U{ch}", [128, NMAT, 128]) for ch in range(NCHK)]
        sums = sb("sums", [128, 2, C])
        top = sb("top", [2 * C, 1])
        diag = sb("diag", [2 * C, 2 * C])
        norms = sb("norms", [128, C])
        scl = sb("scl", [128, 4, C])

        conv_ps = [pb(f"conv_ps{i}", [128, 4, W]) for i in range(2)]
        R_ps = [pb(f"R_ps{s}", [128, NMAT, 128]) for s in range(2)]
        V_ps = [pb(f"V_ps{s}", [128, NMAT, 128]) for s in range(2)]
        win_ps = pb("win_ps", [128, 512])
        row_ps = pb("row_ps", [128, 512])

        s_xsp = sem("x_loaded_by_sp")
        s_xsp1, s_xpool1 = sem("x_1_loaded_by_sp"), sem("x_1_loaded_by_pool")
        s_x1 = sem("x1_rows_loaded")
        s_x1_pool = sem("x1_rows_0_1_loaded_by_pool")
        sB_bn, sB_sum, sB_ve, sB_sd = (sem(f"rows_B_{n}") for n in ("stat", "sum", "var", "sqrt"))
        sC_bn, sC_sum, sC_ve, sC_sd = (sem(f"rows_C_{n}") for n in ("stat", "sum", "var", "sqrt"))
        s_chainB = sem("chain_B")
        s_chainC = sem("chain_rows_C")
        s_DN = sem("DN_ready")
        s_T = sem("transposed")
        s_Gr = sem("gram_ready")
        s_V0 = sem("V0_ready")
        s_abs = sem("abs_sums_ready")
        s_nT = sem("norms_transposed")
        s_dg = sem("diag_ready")
        s_nB = sem("norms_spread")
        s_sc = sem("scales_ready")
        s_V0s = sem("V0_scaled")
        s_R0 = sem("R0_ready")
        s_Rp = sem("R_product")
        s_Vp = sem("V_product")
        s_R = sem("R_ready")
        s_V = sem("V_ready")
        s_U = sem("U_ready")
        s_keep = sem("x1_kept")
        s_xs = sem("x2_stored")
        s_x2 = sem("x2_ready")
        s_ycol = sem("y_column_ready")
        s_y = sem("y_stored")
        s_yrow = sem("y_last_row_stored")
        s_y_pool = sem("y_stored_by_pool")
        s_first, s_last = sem("first_window_fixed"), sem("last_window_fixed")
        s_tail = [sem(f"last_win_D{p}_loaded") for p in range(3)]

        block = ctx.enter_context(nc.Block())

        SP_X, POOL_X = (0, 1, 2, 5), (3, 4)
        SP_ROWS, POOL_ROWS = (0, 2, 3, 5), (1, 4)
        SP_Y, POOL_Y = (0, 2, 4, 5), (1, 3)

        def windows_of(groups):
            return sum(SPLIT_G[g][1] for g in groups)
        n_xs_sp, n_x = windows_of(SP_X), windows_of(POOL_X)
        n_x1, n_x1_pool = NBLK, windows_of(POOL_ROWS)
        n_xs = NCHK + 2
        n_x2 = NG + 1
        n_x3 = 5
        n_y = NBLK

        def x1_moved(b):
            return at(16 * n_x1, b, -16 * n_x1_pool * (1 if isinstance(b, int) and b == 1 else 2))

        def load_x(eng, b, g):
            second = isinstance(b, int) and b == 1
            win = (cA1 if second else cA).win
            by_sp, by_pool = (s_xsp1, s_xpool1) if second else (s_xsp, cA.s_win)
            if second:
                eng.wait_ge(s_zero, 2)
            else:
                wait(eng, cA.s_dl, at(NG, b - 1, g + 1))
            k0, kn = SPLIT_G[g]
            for k in range(k0, k0 + kn):
                h0 = window_row(k)
                lo, hi = max(h0, 0), min(h0 + WIN, H)
                eng.dma_start(win[(lo - h0) * C:(hi - h0) * C, k, :],
                              x[bass.ds(b, 1), :, lo:hi, :].rearrange("b c h w -> (b h) c w"))\
                    .then_inc(by_sp if g in SP_X else by_pool, 16)

        def rows_from_windows(eng, b, g, done=s_x1, first=0):
            if g == first:
                wait(eng, s_keep, at(1, b))
                wait(eng, s_U, at(NCHK, b - 1, 2))
            eng.wait_ge(cA.s_out, at(NG, b, g + 1))
            k0, kn = SPLIT_G[g]
            out = (cA1 if isinstance(b, int) and b == 1 else cA).out
            for k in range(k0, k0 + kn):
                if k < NBLK - 1:
                    eng.dma_start(x1[OUT_ROWS * k:OUT_ROWS * (k + 1), :, :], out[:, k, :])\
                        .then_inc(done, 16)
                else:
                    first_row = FULL - (LAST_ROW + 1)
                    eng.dma_start(x1[FULL:H, :, :], out[first_row * C:OP, k, :]).then_inc(s_x1, 16)

        def store_x2(sp, b, ch):
            if ch == 0:
                wait(sp, cC.s_win, at(16 * n_x2, b))
            sp.wait_ge(s_x2, at(NCHK, b, ch + 1))
            cs = slice(NMAT * ch, NMAT * (ch + 1))
            sp.dma_start(rows_dram[1:H + 1, cs, :], x2[:, cs, :]).then_inc(s_xs, 16)

        def store_x2_edges(sp, b):
            sp.wait_ge(s_x2, at(NCHK, b, NCHK))
            sp.dma_start(rows_dram[0:1, :, :], x2[H - 1:H, :, :]).then_inc(s_xs, 16)
            sp.dma_start(rows_dram[H + 1:H + 2, :, :], x2[0:1, :, :]).then_inc(s_xs, 16)

        def load_x2(sp, b, g):
            if g == 0:
                wait(sp, cC.s_dl, at(NG, b))
                if isinstance(b, int) and b == 0:
                    sp.wait_ge(cA.s_dl, 2 * NG)
                sp.wait_ge(s_xs, at(16 * n_xs, b, 16 * n_xs))
            k0, kn = SPLIT_G[g]
            regular = min(kn, NBLK - 1 - k0)

            def windows(first_row, n):
                return bass.AP(tensor=rows_dram.tensor, offset=rows_dram.offset + first_row * C * W,
                               ap=[[W, WIN * C], [OUT_ROWS * C * W, n], [1, W]])
            sp.dma_start(cC.win[:, k0:k0 + regular, :], windows(OUT_ROWS * k0, regular)).then_inc(cC.s_win, 16)
            if regular < kn:
                sp.dma_start(cC.win[:, NBLK - 1:NBLK, :], windows(LAST_ROW + 1, 1)).then_inc(cC.s_win, 16)

        def windows_from_windows(sp, b):
            sp.wait_ge(cC.s_out, at(NG, b, NG))
            wait(sp, cD.s_dl, at(NG, b))
            o, w, last = cC.out, cD.win, NBLK - 1
            above = window_row(last) - OUT_ROWS * (last - 1)
            below = OUT_ROWS * last - (LAST_ROW + 1)
            sp.dma_start(w[C:C + OP, :, :], o[:, :, :]).then_inc(cD.s_win, 16)
            sp.dma_start(w[0:C, 1:last, :], o[OP - C:OP, 0:last - 1, :]).then_inc(cD.s_win, 16)
            sp.dma_start(w[0:C, last, :], o[above * C:(above + 1) * C, last - 1, :]).then_inc(cD.s_win, 16)
            sp.dma_start(w[(WIN - 1) * C:, 0:last - 1, :], o[0:C, 1:last, :]).then_inc(cD.s_win, 16)
            sp.dma_start(w[(WIN - 1) * C:, last - 1, :], o[below * C:(below + 1) * C, last, :])\
                .then_inc(cD.s_win, 16)

        TAIL = [(k0, k1, min(k1 // SPLIT_G[0][1] + 1, NG)) for k0, k1 in ((0, 9), (9, 18), (18, NBLK))]
        n_tail = [3, 3, 5]

        def windows_from_windows_last(sp):
            o, w, last = cC.out, cD.win, NBLK - 1
            wait(sp, cD.s_dl, at(NG, B - 1))
            for (k0, k1, groups), s in zip(TAIL, s_tail):
                sp.wait_ge(cC.s_out, at(NG, B - 1, groups))
                sp.dma_start(w[C:C + OP, k0:k1, :], o[:, k0:k1, :]).then_inc(s, 16)
                a0, a1 = max(k0, 1), min(k1, last)
                sp.dma_start(w[0:C, a0:a1, :], o[OP - C:OP, a0 - 1:a1 - 1, :]).then_inc(s, 16)
                b1 = min(k1, last - 1)
                sp.dma_start(w[(WIN - 1) * C:, k0:b1, :], o[0:C, k0 + 1:b1 + 1, :]).then_inc(s, 16)
            above = window_row(last) - OUT_ROWS * (last - 1)
            below = OUT_ROWS * last - (LAST_ROW + 1)
            sp.dma_start(w[0:C, last, :], o[above * C:(above + 1) * C, last - 1, :]).then_inc(s_tail[-1], 16)
            sp.dma_start(w[(WIN - 1) * C:, last - 1, :], o[below * C:(below + 1) * C, last, :])\
                .then_inc(s_tail[-1], 16)

        def store_y(sp, b, groups=range(NG), done=None):
            done = done or s_y

            def rows(lo, hi):
                return y[bass.ds(b, 1), :, lo:hi, :].rearrange("b c h w -> (b h) c w")
            wait(sp, s_ycol, at(1, b, 1))
            if 0 in groups:
                sp.dma_start(rows(H - 1, H), cC.out[OP - C:OP, NBLK - 1, :]).then_inc(s_yrow, 16)
            for g in groups:
                k0, kn = SPLIT_G[g]
                wait(sp, cD.s_out, at(NG, b, g + 1))
                for k in reversed(range(k0, k0 + kn)):
                    if k < NBLK - 1:
                        sp.dma_start(rows(OUT_ROWS * k, OUT_ROWS * (k + 1)), cD.out[:, k, :]).then_inc(done, 16)
                    else:
                        first = FULL - (LAST_ROW + 1)
                        sp.dma_start(rows(FULL, H - 1), cD.out[first * C:OP - C, k, :]).then_inc(done, 16)

        def newton(dve, link, inv, ve, sd, t1, t2):
            link(dve.reciprocal(t1, sd))
            link(dve.tensor_tensor(t2, t1, t1, ALU.mult))
            link(dve.tensor_tensor(t2, t2, ve, ALU.mult))
            link(dve.tensor_scalar(t2, t2, -0.5, 1.5, ALU.mult, ALU.add))
            link(dve.tensor_tensor(inv, t1, t2, ALU.mult))

        class Chain:

            def __init__(self, eng, s, per, b, done=0):
                self.eng, self.s, self.per, self.b, self.n = eng, s, per, b, done

            def __call__(self, ins):
                self.n += 1
                ins.then_inc(self.s, 1)
                self.eng.wait_ge(self.s, at(self.per, self.b, self.n))

        MEAN, NEG, VE, SD, T1, T2, INV, OUTB, DEV, ADD, SPARE, PART, SUM = 0, 1, 2, 3, 4, 5, 6, 7, 8, 10, 12, 13, 14

        def col(c, j, n=1, rows=128):
            return c.col[0:rows, j:j + n]

        NWIN_1, NWIN_2, NWIN_3 = 3, 8, 5
        NWIN = NWIN_1 + NWIN_2 + NWIN_3 + 2

        def is_tail(c, b):
            return c is cD and isinstance(b, int) and b == B - 1

        def shares(dve, link, c, b, main, last):
            rows, j = (OP, 2) if is_tail(c, b) else (128, 0)
            link(dve.tensor_tensor(col(c, PART, rows=rows), last, share[0:rows, j + 1:j + 2], ALU.mult))
            dve.scalar_tensor_tensor(col(c, SUM, rows=rows), main, share[0:rows, j:j + 1],
                                     col(c, PART, rows=rows), ALU.mult, ALU.add).then_inc(c.s_stat, 1)

        def win_stats_1(dve, c, b, *parts):
            n, last = (n_x3 if c is cD else n_x), NBLK // 3
            tail = is_tail(c, b)
            rows, src = (OP, cC.out) if tail else (128, c.win)
            for part in parts:
                turn = b if c is cD or (isinstance(b, int) and b == 0) else b - 1
                if c is cA1 and part < 2:
                    dve.wait_ge(*((s_xsp1, 16 * n_xs_sp), (s_xpool1, 16 * n))[part])
                elif c is cA and part == 0:
                    dve.wait_ge(s_xsp, at(16 * n_xs_sp, turn, 16 * n_xs_sp))
                elif not tail and c is not cA1 and part == (1 if c is cA else 0):
                    dve.wait_ge(c.s_win, at(16 * n, turn, 16 * n))
                for j in (range(3), range(3, 6), range(6, last))[part]:
                    if tail:
                        dve.wait_ge(cC.s_out, at(NG, b, (3 * j + 2) // SPLIT_G[0][1] + 1))
                    dve.bn_stats(c.bn[0:rows, j, :], src[:, 3 * j:3 * j + 3, :])
                if part == 2:
                    link = Chain(dve, c.s_chain, NWIN, b)
                    link(dve.bn_stats(c.bn[0:rows, last, :], src[:, NBLK - 1, :]))
                    dve.memset(col(c, SPARE), 0.0)
                    dve.bn_aggr(c.mv[0:rows, 0, :], c.bn[0:rows, 0:last, :])
                    link(dve.bn_aggr(c.mv[0:rows, 1, :], c.bn[0:rows, last, :]))
                    shares(dve, link, c, b, c.mv[0:rows, 0, 0:1], c.mv[0:rows, 1, 0:1])
                    assert link.n == NWIN_1

        def win_stats_2(dve, c, b):
            link = Chain(dve, c.s_chain, NWIN, b, NWIN_1)
            rows = OP if is_tail(c, b) else 128
            dve.wait_ge(c.s_sum, at(2, b, 1))
            link(dve.tensor_copy(col(c, MEAN), win_ps[:, 0:1]))
            dev2 = col(c, DEV, 2, rows=rows)
            link(dve.tensor_scalar(dev2, c.mv[0:rows, :, 0], col(c, MEAN, rows=rows), None, ALU.subtract))
            link(dve.tensor_tensor(dev2, dev2, dev2, ALU.mult))
            link(dve.tensor_tensor(dev2, dev2, c.mv[0:rows, :, 1], ALU.add))
            shares(dve, link, c, b, col(c, DEV, rows=rows), col(c, DEV + 1, rows=rows))
            link(dve.tensor_scalar(col(c, ADD, 2), edge_drop, col(c, MEAN), None, ALU.mult))
            link(dve.tensor_scalar(col(c, NEG), col(c, MEAN), -1.0, None, ALU.mult))
            if is_tail(c, b):
                dve.wait_ge(s_tail[0], 16 * n_tail[0])
            first = dve.tensor_scalar(c.win[:, 0, :], c.win[:, 0, :], edge_keep[:, 0:1], col(c, ADD),
                                      ALU.mult, ALU.add)
            if is_tail(c, b):
                first.then_inc(s_first, 1)
            if c is not cD:
                link(dve.tensor_tensor(col(c, OUTB, rows=OP), col(c, MEAN, rows=OP), bias[:, :], ALU.add))
            else:
                link(dve.tensor_copy(col(c, OUTB), col(c, MEAN)))
            if is_tail(c, b):
                dve.wait_ge(s_first, 1)
                dve.memset(col(c, SPARE), 0.0).then_inc(c.s_fix, 1)
            else:
                last_window(dve, c).then_inc(c.s_fix, 1)
            assert link.n == NWIN_1 + NWIN_2

        def last_window(dve, c):
            return dve.tensor_scalar(c.win[:, NBLK - 1, :], c.win[:, NBLK - 1, :], edge_keep[:, 1:2],
                                     col(c, ADD + 1), ALU.mult, ALU.add)

        def win_stats_3(dve, c, b):
            link = Chain(dve, c.s_chain, NWIN, b, NWIN_1 + NWIN_2)
            dve.wait_ge(c.s_sum, at(2, b, 2))
            dve.tensor_scalar(col(c, VE), win_ps[:, 1:2], EPS, None, ALU.add).then_inc(c.s_ve, 1)
            dve.wait_ge(c.s_sd, at(1, b, 1))
            newton(dve, link, col(c, INV), col(c, VE), col(c, SD), col(c, T1), col(c, T2))

        def win_weights(dve, c, b):
            conv_weights(dve, Chain(dve, c.s_chain, NWIN, b, NWIN - 2), c, b, col(c, INV))

        def conv_weights(dve, link, c, b, inv):
            if c is not cA1:
                wait(dve, c.s_acc, at(NG, b))
            if c is cC and isinstance(b, int) and b == 0:
                dve.wait_ge(cA.s_acc, 2 * NG)
            link(dve.scalar_tensor_tensor(c.scaled[:, :], c.base[:, :], inv, residual, ALU.mult, ALU.add))
            link(dve.tensor_copy(c.w[:, 0, :], c.scaled[:, :]))
            dve.tensor_tensor(c.w[:, 1, :], c.scaled[:, :], c.w[:, 0, :].bitcast(f32), ALU.subtract)\
                .then_inc(c.s_w, 1)

        def low_parts(dve, c, b, g):
            k0, kn = SPLIT_G[g]
            dve.wait_ge(c.s_dh, at(NG, b, g + 1))
            dve.scalar_tensor_tensor(c.d[:, 1, k0:k0 + kn, 1:W + 1], c.win[:, k0:k0 + kn, :], col(c, MEAN),
                                     c.d[:, 0, k0:k0 + kn, 1:W + 1].bitcast(f32),
                                     ALU.subtract, ALU.subtract).then_inc(c.s_dl, 1)

        def high_parts(act, c, b, g):
            k0, kn = SPLIT_G[g]
            if c is cD:
                if isinstance(b, int) and b + 2 >= B:
                    act.wait_ge(cA.s_acc, at(NG, B))
                else:
                    act.wait_ge(cA.s_acc, at(NG, b + 2, g + 1))
            if is_tail(c, b) and g == 2:
                act.wait_ge(s_tail[1], 16 * n_tail[1])
            if is_tail(c, b) and g == 4:
                act.wait_ge(s_tail[2], 16 * n_tail[2])
            if is_tail(c, b) and g == 5:
                act.wait_ge(s_last, 1)
            if g == 0:
                act.wait_ge(c.s_fix, at(1, b, 1))
                if c is not cA1:
                    wait(act, c.s_acc, at(NG, b))
                if c is cC and isinstance(b, int) and b == 0:
                    act.wait_ge(cA.s_acc, 2 * NG)
                if c is cA:
                    wait(act, cD.s_acc, at(NG, b - 2))
                if c is cC:
                    act.wait_ge(c.s_win, at(16 * n_x2, b, 16 * n_x2))
            act.activation(c.d[:, 0, k0:k0 + kn, 1:W + 1], c.win[:, k0:k0 + kn, :], ACT.Identity,
                           bias=col(c, NEG)).then_inc(c.s_dh, 1)

        def win_mean(pe, c, b):
            rows = OP if is_tail(c, b) else 128
            pe.wait_ge(c.s_stat, at(2, b, 1))
            pe.matmul(win_ps[:, 0:1], same_group[0:rows, :], col(c, SUM, rows=rows), start=True, stop=True)\
                .then_inc(c.s_sum, 1)

        def win_var(pe, c, b):
            rows = OP if is_tail(c, b) else 128
            pe.wait_ge(c.s_stat, at(2, b, 2))
            pe.matmul(win_ps[:, 1:2], same_group[0:rows, :], col(c, SUM, rows=rows), start=True, stop=True)\
                .then_inc(c.s_sum, 1)

        NROW = 4 + 5

        def row_stats_1(dve, rows, s_bn, half):
            for g in range(half * G // 2, (half + 1) * G // 2):
                ins = dve.bn_stats(st[:, g, :], rows[:, GC * g:GC * (g + 1), :])
            if half == 1:
                ins.then_inc(s_bn, 1)

        def row_stats_2(dve, link, s_bn, s_sum, t, b):
            mean = t[:, 0, :]
            halves = st[:, :, :].rearrange("p g (a t) -> p (g a) t", t=3)
            dve.wait_ge(s_bn, at(2, b, 1))
            dve.wait_ge(s_sum, at(2, b, 1))
            link(dve.tensor_reduce(mean, row_ps[:, 0:2 * G].rearrange("p (g a) -> p g a", a=2), AX.X, ALU.add))
            d, sq = dev[:, 0, :], dev[:, 1, :]
            link(dve.tensor_tensor(d.rearrange("p (g a) -> p g a", a=2),
                                   halves[:, :, 1].rearrange("p (g a) -> p g a", a=2),
                                   mean.unsqueeze(2).broadcast_to([128, G, 2]), ALU.subtract))
            link(dve.scalar_tensor_tensor(sq, d, float(GC * W // 2), d, ALU.mult, ALU.mult))
            dve.tensor_tensor(sq, sq, halves[:, :, 2], ALU.add).then_inc(s_bn, 1)

        def row_stats_3(dve, link, s_sum, s_ve, t, b):
            dve.wait_ge(s_sum, at(2, b, 2))
            link(dve.tensor_reduce(t[:, 4, :], row_ps[:, 2 * G:4 * G].rearrange("p (g a) -> p g a", a=2),
                                   AX.X, ALU.add))
            dve.tensor_scalar(t[:, 2, :], t[:, 4, :], EPS, None, ALU.add).then_inc(s_ve, 1)

        def row_stats_4(dve, link, s_sd, t, b):
            dve.wait_ge(s_sd, at(1, b, 1))
            newton(dve, link, t[:, 1, :], t[:, 2, :], t[:, 3, :], t[:, 4, :], t[:, 5, :])

        def row_mean(pe, s_bn, s_sum, b):
            pe.wait_ge(s_bn, at(2, b, 1))
            pe.matmul(row_ps[:, 0:2 * G], ones_mean[:, :],
                      st[:, :, :].rearrange("p g (a t) -> p (g a) t", t=3)[:, :, 1],
                      start=True, stop=True).then_inc(s_sum, 1)

        def row_var(pe, s_bn, s_sum, b):
            pe.wait_ge(s_bn, at(2, b, 2))
            pe.matmul(row_ps[:, 2 * G:4 * G], ones_var[:, :], dev[:, 1, :], start=True, stop=True)\
                .then_inc(s_sum, 1)

        def conv_group(pe, c, b, g, prev, beside=False):
            k0, kn = SPLIT_G[g]
            if g == 0:
                pe.wait_ge(c.s_w, at(1, b, 1))
            pe.wait_ge(c.s_dl, at(NG, b, g + 1))
            if c is cC:
                pe.wait_ge(s_pad, at(NG, b, g + 1))
            if beside and g < 2:
                pe.wait_ge(s_V0, at(NCHK, b + 1, 2 + g + 1))
            elif g >= 2:
                pe.wait_ge(c.s_out, at(NG, b, g - 1))
            elif prev is not None:
                pe.wait_ge(prev[0].s_out, at(NG, prev[1], NG - 1 + g))
            n = 0
            for dx in range(TAPS):
                for wp, dp in ((0, 0), (0, 1), (1, 0)):
                    ins = pe.matmul(conv_ps[g % 2][0:OP, 0:kn, :], c.w[:, wp, dx * OP:(dx + 1) * OP],
                                    c.d[:, dp, k0:k0 + kn, dx:dx + W], start=n == 0, stop=n == 8)
                    n += 1
            ins.then_inc(c.s_acc, 1)

        def conv_out(act, c, b, g):
            k0, kn = SPLIT_G[g]
            act.wait_ge(c.s_acc, at(NG, b, g + 1))
            if g == 0:
                if c is cA and not (isinstance(b, int) and b == 0):
                    act.wait_ge(s_x1, x1_moved(b))
                if c is cC and isinstance(b, int) and b == 0:
                    act.wait_ge(s_x1, x1_moved(2))
                    act.wait_ge(s_x1_pool, 2 * 16 * n_x1_pool)
                if c is cC:
                    wait(act, cD.s_win, at(16 * n_x3, b))
                    wait(act, s_ycol, at(1, b))
                    wait(act, s_yrow, at(16, b))
                if c is cD:
                    wait(act, s_y, at(16 * n_y, b))
            wn = W - 1 if c is cD else W
            act.activation(c.out[:, k0:k0 + kn, 0:wn], conv_ps[g % 2][0:OP, 0:kn, 0:wn], ACT.Identity,
                           bias=col(c, OUTB, rows=OP)).then_inc(c.s_out, 1)

        def copy_column(pool, out, in_):
            p, *n = out.shape
            ones = ones_all[0:p, 0:int(np.prod(n))]
            if len(n) == 3:
                ones = ones.rearrange("p (a k o) -> p a k o", a=n[0], o=1)
            else:
                ones = ones.unsqueeze(2)
            return pool.tensor_tensor(out, in_, ones, ALU.mult)

        def y_column(pool, i):
            pool.wait_ge(cC.s_out, at(NG, i, NG))
            wait(pool, s_y, at(16 * n_y, i))
            copy_column(pool, cD.out[:, :, W - 1:W], cC.out[:, :, W - 1:W]).then_inc(s_ycol, 1)

        per_R = NCHK * (STEPS - 1)
        per_V = NCHK * (STEPS - 1)
        per_Vp = NCHK * STEPS
        T_ps = [V_ps[0], V_ps[1], conv_ps[0], conv_ps[1]]

        def n_R(r, k, s):
            return 2 * (STEPS - 1) * r + 2 * k + s + 1

        def n_Vp(r, k, s):
            return 2 * STEPS * r + 2 * k + s + 1

        def sp_cycle(sp, i, prev, nxt, nxt2):
            if prev:
                windows_from_windows(sp, i - 1)
            if prev and nxt2:
                for g in SP_X:
                    load_x(sp, i + 2, g)
            store_x2(sp, i, 0)
            store_x2(sp, i, 1)
            if nxt:
                for g in range(NG):
                    if prev or g not in POOL_ROWS:
                        rows_from_windows(sp, i + 1, g)
            store_x2(sp, i, 2)
            store_x2(sp, i, 3)
            store_x2_edges(sp, i)
            for g in range(NG):
                load_x2(sp, i, g)
            if prev:
                store_y(sp, i - 1)

        def pe_gram(pe, b, ch):
            s = ch % 2
            if ch >= 2:
                pe.wait_ge(s_R, at(per_R, b, n_R(0, STEPS - 2, s)))
            for m in range(NMAT):
                ins = pe.matmul(R_ps[s][:, m, :], DN[:, NMAT * ch + m, :], DN[:, NMAT * ch + m, :],
                                start=True, stop=True)
            ins.then_inc(s_Gr, 1)

        def pe_norms(pe, b, prev, nxt):
            wait(pe, s_x2, at(NCHK, b))
            for ch in range(NCHK):
                if ch == NCHK - 1:
                    pe_gram(pe, b, 0)
                pe.wait_ge(s_DN, at(NCHK, b, ch + 1))
                if ch >= 2:
                    if isinstance(b, int) and b < 2:
                        pe.wait_ge(cA.s_out, at(NG, 1, NG + ch - 3))
                    else:
                        pe.wait_ge(cD.s_out, at(NG, b - 2, NG + ch - 3))
                for m in range(NMAT):
                    ins = pe.transpose(T_ps[ch][:, m, :], DN[:, NMAT * ch + m, :], ident)
                ins.then_inc(s_T, 1)
            pe_gram(pe, b, 1)
            for g in range(NG):
                if nxt and prev and g == 1:
                    win_mean(pe, cA, b + 1)
                if prev:
                    conv_group(pe, cC, b - 1, g, None, True)
                if g == 2:
                    pe.wait_ge(s_abs, at(1, b, 1))
                    pe.transpose(row_ps[0:2 * C, 128:256], sums[:, :, :].rearrange("p a c -> p (a c)"), ident)\
                        .then_inc(s_nT, 1)
                if g == 3:
                    pe.wait_ge(s_dg, at(1, b, 1))
                    pe.matmul(row_ps[:, 256:256 + 2 * C], ones_all[0:2 * C, :], diag[:, :],
                              start=True, stop=True).then_inc(s_nB, 1)

        def pe_step(pe, b, r, k):
            for s in range(2):
                ch = 2 * r + s
                Rk = R[s][(k + r) % 2]
                if k == 0:
                    pe.wait_ge(s_R0, at(NCHK, b, ch + 1))
                    pe.wait_ge(s_V0, at(NCHK, b, ch + 1))
                    if r > 0:
                        pe.wait_ge(s_x2, at(NCHK, b, ch - 1))
                else:
                    pe.wait_ge(s_R, at(per_R, b, n_R(r, k - 1, s)))
                if k < STEPS - 1:
                    for m in range(NMAT):
                        ins = pe.matmul(R_ps[s][:, m, :], Rk[:, m, :], Rk[:, m, :], start=True, stop=True)
                    ins.then_inc(s_Rp, 1)
                elif r + 1 < ROUNDS:
                    pe_gram(pe, b, ch + 2)
                if k > 0:
                    pe.wait_ge(s_V, at(per_V, b, n_R(r, k - 1, s)))
                for m in range(NMAT):
                    ins = pe.matmul(V_ps[s][:, m, :], Rk[:, m, :], V[ch][:, m, :], start=True, stop=True)
                ins.then_inc(s_Vp, 1)

        def pe_cycle(pe, i, prev, nxt, nxt2):
            pe_norms(pe, i, prev, nxt)
            if nxt and prev:
                win_var(pe, cA, i + 1)
            for k in range(STEPS):
                pe_step(pe, i, 0, k)
            for g in range(NG):
                if prev and nxt:
                    conv_group(pe, cA, i + 1, g, (cC, i - 1))
                if prev and nxt and g == 2:
                    win_mean(pe, cD, i - 1)
                if prev and nxt and g == 4:
                    win_var(pe, cD, i - 1)
            for k in range(STEPS):
                pe_step(pe, i, 1, k)
                if not nxt and k == 0:
                    win_mean(pe, cD, i - 1)
                if not nxt and k == 1:
                    win_var(pe, cD, i - 1)
                if nxt and k == (3 if prev else 4):
                    row_mean(pe, sB_bn, sB_sum, i + 1)
            if nxt:
                row_var(pe, sB_bn, sB_sum, i + 1)
            for g in range(NG):
                if prev:
                    conv_group(pe, cD, i - 1, g, (cA, i + 1) if nxt else (cC, i - 1))
                if g == 2:
                    row_mean(pe, sC_bn, sC_sum, i)
                if g == 3:
                    row_var(pe, sC_bn, sC_sum, i)

        def pe_end(pe):
            i = B - 1
            for g in range(NG):
                conv_group(pe, cC, i, g, (cD, i - 1))
            win_mean(pe, cD, i)
            win_var(pe, cD, i)
            for g in range(NG):
                conv_group(pe, cD, i, g, (cC, i))

        def act_sqrt(act, s_ve, s_sd, out, in_, b):
            act.wait_ge(s_ve, at(1, b, 1))
            act.activation(out, in_, ACT.Sqrt).then_inc(s_sd, 1)

        def act_norms(act, b, prev, nxt):
            for ch in range(NCHK):
                act.wait_ge(s_T, at(NCHK, b, ch + 1))
                act.activation(V[ch][:, :, :], T_ps[ch][:, :, :], ACT.Copy).then_inc(s_V0, 1)
            for g in range(NG):
                if prev and g < 2:
                    high_parts(act, cC, b - 1, 2 + 2 * g)
                    high_parts(act, cC, b - 1, 3 + 2 * g)
                if prev:
                    conv_out(act, cC, b - 1, g)
                if nxt and prev and g >= 3:
                    high_parts(act, cA, b + 1, g - 3)

        def act_step(act, b, r, k, s):
            act.wait_ge(s_Rp, at(per_R, b, n_R(r, k, s)))
            if k > 0:
                act.wait_ge(s_Vp, at(per_Vp, b, n_Vp(r, k - 1, s)))
            act.activation(R[s][(k + 1 + r) % 2][:, :, :], R_ps[s][:, :, :], ACT.Copy).then_inc(s_R, 1)

        def win_sqrt(act, c, b):
            act_sqrt(act, c.s_ve, c.s_sd, col(c, SD), col(c, VE), b)

        def keep_x1(act, b):
            wait(act, s_xs, at(16 * n_xs, b))
            c1 = NMAT * NCHK // 2
            act.activation(x2[:, c1:C, :], x1[:, c1:C, :], ACT.Copy).then_inc(s_keep, 1)

        def act_cycle(act, i, prev, nxt, nxt2):
            act_norms(act, i, prev, nxt)
            for k in range(STEPS - 1):
                act_step(act, i, 0, k, 0)
                act_step(act, i, 0, k, 1)
                if nxt and prev and k == 0:
                    win_sqrt(act, cA, i + 1)
                    high_parts(act, cA, i + 1, 3)
                if nxt and prev and k == 1:
                    high_parts(act, cA, i + 1, 4)
                    high_parts(act, cA, i + 1, 5)
                if k == 2:
                    keep_x1(act, i)
            for g in range(NG):
                if nxt and prev:
                    conv_out(act, cA, i + 1, g)
                if nxt and prev and g == 4:
                    win_sqrt(act, cD, i - 1)
            for k in range(STEPS - 1):
                act_step(act, i, 1, k, 0)
                act_step(act, i, 1, k, 1)
                if prev:
                    if k == 2 and not nxt:
                        win_sqrt(act, cD, i - 1)
                    if k >= 1:
                        high_parts(act, cD, i - 1, 2 * k - 2)
                        high_parts(act, cD, i - 1, 2 * k - 1)
            for g in range(NG):
                if prev:
                    conv_out(act, cD, i - 1, g)
                if nxt and g == 0:
                    act_sqrt(act, sB_ve, sB_sd, tB[:, 3, :], tB[:, 2, :], i + 1)
                if g == 3:
                    act_sqrt(act, sC_ve, sC_sd, tC[:, 3, :], tC[:, 2, :], i)
            high_parts(act, cC, i, 0)
            high_parts(act, cC, i, 1)

        def act_end(act):
            i = B - 1
            for g in range(2, NG):
                high_parts(act, cC, i, g)
            for g in range(NG):
                conv_out(act, cC, i, g)
            win_sqrt(act, cD, i)
            for g in range(NG):
                high_parts(act, cD, i, g)
            for g in range(NG):
                conv_out(act, cD, i, g)

        NROW_B = NROW + 1
        perB = NROW_B + 5
        perRC = NROW + 7

        def dve_norms(dve, b, prev, nxt):
            link = Chain(dve, s_chainB, perB, b, NROW_B)
            for ch in range(NCHK):
                dve.wait_ge(s_DN, at(NCHK, b, ch + 1))
                dve.tensor_reduce(sums[:, 0, NMAT * ch:NMAT * (ch + 1)], DN[:, NMAT * ch:NMAT * (ch + 1), :],
                                  AX.X, ALU.add, apply_absolute_value=True)
            if prev:
                low_parts(dve, cC, b - 1, 2)
                low_parts(dve, cC, b - 1, 3)
            for ch in range(NCHK):
                dve.wait_ge(s_V0, at(NCHK, b, ch + 1))
                ins = dve.tensor_reduce(sums[:, 1, NMAT * ch:NMAT * (ch + 1)], V[ch][:, :, :],
                                        AX.X, ALU.add, apply_absolute_value=True)
            ins.then_inc(s_abs, 1)
            if prev:
                low_parts(dve, cC, b - 1, 4)
                low_parts(dve, cC, b - 1, 5)
            dve.wait_ge(s_nT, at(1, b, 1))
            link(dve.tensor_reduce(top[:, :], row_ps[0:2 * C, 128:256], AX.X, ALU.max))
            dve.tensor_scalar(diag[:, :], ident[0:2 * C, 0:2 * C], top[:, :], None, ALU.mult)\
                .then_inc(s_dg, 1)
            if nxt and prev:
                win_stats_2(dve, cA, b + 1)
            dve.wait_ge(s_nB, at(1, b, 1))
            link(dve.tensor_copy(norms[:, :], row_ps[:, 256:256 + C]))
            link(dve.tensor_tensor(scl[:, 0, :], norms[:, :], row_ps[:, 256 + C:256 + 2 * C], ALU.mult))
            link(dve.reciprocal(scl[:, 1, :], scl[:, 0, :]))
            dve_R0(dve, b, 0)
            link(dve.tensor_tensor(scl[:, 2, :].rearrange("p (g a) -> p g a", a=GC),
                                   scl[:, 1, :].rearrange("p (g a) -> p g a", a=GC),
                                   tB[:, 4, :].unsqueeze(2).broadcast_to([128, G, GC]), ALU.mult))
            dve.tensor_scalar(scl[:, 3, :], scl[:, 2, :], -1.0, None, ALU.mult).then_inc(s_sc, 1)
            dve_R0(dve, b, 1)

        def dve_R0(dve, b, ch):
            s = ch % 2
            dve.wait_ge(s_Gr, at(NCHK, b, ch + 1))
            if ch >= 2:
                dve.wait_ge(s_Vp, at(per_Vp, b, n_Vp(0, STEPS - 2, s)))
            for m in range(NMAT):
                ins = dve.scalar_tensor_tensor(R[s][ch // 2][:, m, :], R_ps[s][:, m, :],
                                               scl[:, 1, NMAT * ch + m:NMAT * ch + m + 1], ident,
                                               ALU.mult, ALU.subtract)
            ins.then_inc(s_R0, 1)

        def dve_step(dve, b, r, k, s):
            ch = 2 * r + s
            dve.wait_ge(s_Vp, at(per_Vp, b, n_Vp(r, k, s)))
            if k == 0:
                dve.wait_ge(s_V0s, at(NCHK, b, ch + 1))
                if ch == 0:
                    dve.wait_ge(s_sc, at(1, b, 1))
                for m in range(NMAT):
                    ins = dve.scalar_tensor_tensor(V[ch][:, m, :], V_ps[s][:, m, :],
                                                   scl[:, 3, NMAT * ch + m:NMAT * ch + m + 1],
                                                   U[ch][:, m, :], ALU.mult, ALU.add)
                ins.then_inc(s_V, 1)
            elif k < STEPS - 1:
                dve.wait_ge(s_V, at(per_V, b, n_R(r, k - 1, s)))
                dve.tensor_tensor(V[ch][:, :, :], V_ps[s][:, :, :], V[ch][:, :, :], ALU.add).then_inc(s_V, 1)
            else:
                dve.wait_ge(s_U, at(NCHK, b, ch + 1))
                if ch == 0:
                    wait(dve, s_xs, at(16 * n_xs, b))
                dve.tensor_tensor(x2[:, NMAT * ch:NMAT * (ch + 1), :], V_ps[s][:, :, :],
                                  U[ch][:, :, :], ALU.add).then_inc(s_x2, 1)

        def dve_rows_C_mean(dve, link, b):
            row_stats_2(dve, link, sC_bn, sC_sum, tC, b)
            link(dve.tensor_tensor(pick[:, 0, :], tC[:, 0, :], onehot, ALU.mult))
            link(dve.tensor_reduce(col(cC, MEAN), pick[:, 0, :], AX.X, ALU.add))
            dve.tensor_scalar(col(cC, NEG), col(cC, MEAN), -1.0, None, ALU.mult).then_inc(cC.s_fix, 1)
            link(dve.tensor_copy(col(cC, OUTB), col(cC, MEAN)))

        def dve_rows_C_weights(dve, link, b):
            row_stats_4(dve, link, sC_sd, tC, b)
            link(dve.tensor_tensor(pick[:, 1, :], tC[:, 1, :], onehot, ALU.mult))
            link(dve.tensor_reduce(col(cC, INV), pick[:, 1, :], AX.X, ALU.add))
            conv_weights(dve, link, cC, b, col(cC, INV))
            assert link.n == perRC, link.n

        def dve_rows_B_end(dve, link, b):
            row_stats_4(dve, link, sB_sd, tB, b)
            link(dve.tensor_tensor(tB[:, 4, :], tB[:, 2, :], tB[:, 1, :], ALU.mult))
            assert link.n == NROW_B, link.n

        def stationary(dve, c, dy):
            base = c.base[:, :].rearrange("p (x r c) -> p x r c", x=TAPS, r=OUT_ROWS)
            tmp = c.scaled[:, :].rearrange("p (x r c) -> p x r c", x=TAPS, r=OUT_ROWS)
            n = (cA, cC, cD).index(c) * (2 * TAPS - 1) + (2 * dy if dy else 1)
            dve.tensor_tensor(
                tmp if dy else base,
                c.compact[:, dy, :, :].unsqueeze(2).broadcast_to([128, TAPS, OUT_ROWS, C]),
                tap_mask[:, dy, :].unsqueeze(1).unsqueeze(3).broadcast_to([128, TAPS, OUT_ROWS, C]),
                ALU.mult).then_inc(s_toep, 1)
            dve.wait_ge(s_toep, n)
            if dy:
                dve.tensor_tensor(base, base, tmp, ALU.add).then_inc(s_toep, 1)
                dve.wait_ge(s_toep, n + 1)

        def dve_cycle(dve, i, prev, nxt, nxt2):
            dve_norms(dve, i, prev, nxt)
            if nxt and prev:
                low_parts(dve, cA, i + 1, 0)
                low_parts(dve, cA, i + 1, 1)
            for k in range(STEPS):
                for s in range(2):
                    dve_step(dve, i, 0, k, s)
                    if not prev and 1 <= k < 1 + TAPS:
                        step = 2 * (k - 1) + s
                        stationary(dve, (cC, cD)[step // TAPS], step % TAPS)
                    if nxt and (k, s) == (0, 1) and prev:
                        win_stats_3(dve, cA, i + 1)
                    if nxt and (k, s) == (1, 0) and prev:
                        win_weights(dve, cA, i + 1)
                    if nxt and prev and (1, 1) <= (k, s) <= (3, 0):
                        low_parts(dve, cA, i + 1, 2 * k + s - 1)
                    if prev and (k, s) == (3, 1):
                        win_stats_1(dve, cD, i - 1, 0)
            if prev and nxt:
                win_stats_1(dve, cD, i - 1, 1, 2)
            dve_R0(dve, i, 2)
            dve_R0(dve, i, 3)
            if prev and nxt:
                win_stats_2(dve, cD, i - 1)
            if nxt2:
                win_stats_1(dve, cA, i + 2, 0)
            if prev and nxt:
                win_stats_3(dve, cD, i - 1)
                win_weights(dve, cD, i - 1)
            if not nxt:
                win_stats_1(dve, cD, i - 1, 1, 2)
            for k in range(STEPS):
                for s in range(2):
                    dve_step(dve, i, 1, k, s)
                    if nxt2 and (k, s) in ((0, 1), (1, 0)):
                        win_stats_1(dve, cA, i + 2, 1 + k)
                    if not prev and (k, s) == (3, 0):
                        dve.wait_ge(s_x1, x1_moved(i + 2))
                        dve.wait_ge(s_x1_pool, 2 * 16 * n_x1_pool)
                        row_stats_1(dve, x1, sB_bn, 0)
                    if not prev and (k, s) == (3, 1):
                        row_stats_1(dve, x1, sB_bn, 1)
                    if prev and nxt and (k, s) == (1, 1):
                        dve.wait_ge(s_x1, x1_moved(i + 2))
                        row_stats_1(dve, x1, sB_bn, 0)
                    if prev and nxt and (k, s) == (2, 0):
                        row_stats_1(dve, x1, sB_bn, 1)
                    if not nxt and (k, s) == (1, 0):
                        win_stats_2(dve, cD, i - 1)
                    if not nxt and (k, s) == (2, 1):
                        win_stats_3(dve, cD, i - 1)
                    if not nxt and (k, s) == (3, 0):
                        win_weights(dve, cD, i - 1)
                    if prev and (k, s) == (2, 1):
                        low_parts(dve, cD, i - 1, 0)
                    if prev and nxt and (k, s) == (3, 1):
                        link_B = Chain(dve, s_chainB, perB, i + 1)
                        row_stats_2(dve, link_B, sB_bn, sB_sum, tB, i + 1)
                    if prev and (k, s) == (3, 1):
                        low_parts(dve, cD, i - 1, 1)
                    if prev and (k, s) == (4, 0):
                        low_parts(dve, cD, i - 1, 2)
            if not prev:
                link_B = Chain(dve, s_chainB, perB, i + 1)
                row_stats_2(dve, link_B, sB_bn, sB_sum, tB, i + 1)
                dve.wait_ge(sB_bn, at(2, i + 1, 2))
            dve.wait_ge(s_x2, at(NCHK, i, NCHK))
            row_stats_1(dve, x2, sC_bn, 0)
            if nxt:
                row_stats_3(dve, link_B, sB_sum, sB_ve, tB, i + 1)
            row_stats_1(dve, x2, sC_bn, 1)
            if prev:
                low_parts(dve, cD, i - 1, 3)
                low_parts(dve, cD, i - 1, 4)
            link = Chain(dve, s_chainC, perRC, i)
            dve_rows_C_mean(dve, link, i)
            if prev:
                low_parts(dve, cD, i - 1, 5)
            row_stats_3(dve, link, sC_sum, sC_ve, tC, i)
            if nxt:
                dve_rows_B_end(dve, link_B, i + 1)
            dve_rows_C_weights(dve, link, i)
            low_parts(dve, cC, i, 0)
            low_parts(dve, cC, i, 1)

        def dve_end(dve):
            for g in range(2, NG):
                low_parts(dve, cC, B - 1, g)
            win_stats_1(dve, cD, B - 1, 0, 1, 2)
            win_stats_2(dve, cD, B - 1)
            win_stats_3(dve, cD, B - 1)
            win_weights(dve, cD, B - 1)
            for g in range(NG):
                if g == 4:
                    dve.wait_ge(s_tail[2], 16 * n_tail[2])
                    last_window(dve, cD).then_inc(s_last, 1)
                if g == 5:
                    dve.wait_ge(s_last, 1)
                low_parts(dve, cD, B - 1, g)

        def pool_DN(pool, b):
            pool.wait_ge(sB_bn, at(2, b, 2))
            wait(pool, s_Gr, at(NCHK, b))
            for ch in range(NCHK):
                gs = slice(ch * NMAT // GC, (ch + 1) * NMAT // GC)
                pool.tensor_tensor(
                    DN[:, NMAT * ch:NMAT * (ch + 1), :].rearrange("p (g a) w -> p g (a w)", a=GC),
                    x1[:, NMAT * ch:NMAT * (ch + 1), :].rearrange("p (g a) w -> p g (a w)", a=GC),
                    tB[:, 0, gs].unsqueeze(2).broadcast_to([128, NMAT // GC, GC * W]),
                    ALU.subtract).then_inc(s_DN, 1)

        def pool_pads(pool, b, *groups):
            for g in groups:
                k0, kn = SPLIT_G[g]
                pool.wait_ge(cC.s_dl, at(NG, b, g + 1))
                d = cC.d[:, :, k0:k0 + kn, :]
                copy_column(pool, d[:, :, :, 0:1], d[:, :, :, W:W + 1].bitcast(f32))
                copy_column(pool, d[:, :, :, W + 1:W + 2], d[:, :, :, 1:2].bitcast(f32)).then_inc(s_pad, 1)

        def pool_add(pool, b, ch):
            pool.wait_ge(s_V, at(per_V, b, n_R(ch // 2, STEPS - 2, ch % 2)))
            if ch == 2:
                pool.wait_ge(s_keep, at(1, b, 1))
            kept = x1 if ch < 2 else x2
            pool.tensor_tensor(U[ch][:, :, :], V[ch][:, :, :], kept[:, NMAT * ch:NMAT * (ch + 1), :],
                               ALU.add).then_inc(s_U, 1)

        def pool_cycle(pool, i, prev, nxt, nxt2):
            if prev:
                pool_pads(pool, i - 1, 2, 3, 4, 5)
            for ch in range(NCHK):
                pool.wait_ge(s_sc, at(1, i, 1))
                pool.tensor_tensor(U[ch][:, :, :], V[ch][:, :, :],
                                   scl[:, 2, NMAT * ch:NMAT * (ch + 1)].unsqueeze(2)
                                   .broadcast_to([128, NMAT, 128]), ALU.mult).then_inc(s_V0s, 1)
            if prev:
                y_column(pool, i - 1)
            pool_add(pool, i, 0)
            pool_add(pool, i, 1)
            if not prev:
                for g in POOL_ROWS:
                    rows_from_windows(pool, i + 1, g, s_x1_pool, POOL_ROWS[0])
            elif nxt2:
                for g in POOL_X:
                    load_x(pool, i + 2, g)
            pool_add(pool, i, 2)
            pool_add(pool, i, 3)
            if nxt:
                pool_DN(pool, i + 1)
            pool_pads(pool, i, 0, 1)

        def cycles(eng, cycle):
            cycle(eng, 0, False, True, True)
            cycle(eng, 1, True, True, True)
            with eng.Fori(2, B - 2) as i:
                cycle(eng, i, True, True, True)
            cycle(eng, B - 2, True, True, False)
            cycle(eng, B - 1, True, False, False)

        def load_taps(sp, c):
            sp.dma_start(c.compact[:, :, :, :].rearrange("p y x c -> p (y x c)"),
                         bass.AP(tensor=c.weights.tensor, offset=c.weights.offset,
                                 ap=[[0, WIN], [TAPS * TAPS * C, C], [1, TAPS * TAPS * C]]))\
                .then_inc(s_wld if c is cA else s_wrest, 16)

        @block.sync
        def _(sp):
            sp.dma_start(cst[:, :], consts).then_inc(s_cst, 16)
            load_taps(sp, cA)
            sp.wait_ge(s_zero, 1)
            for g in SP_X:
                load_x(sp, 0, g)
            load_taps(sp, cC)
            load_taps(sp, cD)
            sp.dma_start(bias[:, :], bass.AP(tensor=b0.tensor, offset=b0.offset,
                                             ap=[[0, OUT_ROWS], [1, C], [1, 1]])).then_inc(s_wrest, 16)
            for g in SP_X:
                load_x(sp, 1, g)
            for g in SP_ROWS:
                rows_from_windows(sp, 0, g)
            for g in SP_X:
                load_x(sp, 2, g)
            cycles(sp, sp_cycle)
            windows_from_windows_last(sp)
            store_y(sp, B - 1, SP_Y)
            sp.wait_ge(s_y, 16 * (n_y * B - windows_of(POOL_Y)))
            sp.wait_ge(s_yrow, 16 * B)

        @block.gpsimd
        def _(pool):
            pool.wait_ge(s_zero, 1)
            for g in POOL_X:
                load_x(pool, 0, g)
            pool.memset(ones_mean[:, :], 1.0 / (GC * W)).then_inc(s_init, 1)
            pool.memset(ones_var[:, :], 1.0 / (GC * H * W)).then_inc(s_init, 1)
            pool.memset(ones_all[:, :], 1.0).then_inc(s_init, 1)
            for c in (cA, cA1):
                pool.memset(c.d[:, :, :, 0:1].bitcast(f32), 0.0).then_inc(s_init, 1)
                pool.memset(c.d[:, :, :, W + 1:W + 2].bitcast(f32), 0.0).then_inc(s_init, 1)
            for g in POOL_X:
                load_x(pool, 1, g)
            for g in POOL_ROWS:
                rows_from_windows(pool, 0, g, s_x1_pool)
            pool_DN(pool, 0)
            for g in POOL_X:
                load_x(pool, 2, g)
            cycles(pool, pool_cycle)
            pool_pads(pool, B - 1, 2, 3, 4, 5)
            y_column(pool, B - 1)
            store_y(pool, B - 1, POOL_Y, s_y_pool)
            pool.wait_ge(s_y_pool, 16 * windows_of(POOL_Y))

        @block.scalar
        def _(act):
            win_sqrt(act, cA, 0)
            for g in range(NG):
                high_parts(act, cA, 0, g)
            for g in range(NG):
                conv_out(act, cA, 0, g)
                if g == 3:
                    win_sqrt(act, cA1, 1)
                    high_parts(act, cA1, 1, 0)
                    high_parts(act, cA1, 1, 1)
                if g == 4:
                    high_parts(act, cA1, 1, 2)
            for g in range(3, NG):
                high_parts(act, cA1, 1, g)
            for g in range(NG):
                conv_out(act, cA1, 1, g)
                if g == 5:
                    act_sqrt(act, sB_ve, sB_sd, tB[:, 3, :], tB[:, 2, :], 0)
            cycles(act, act_cycle)
            act_end(act)

        def first_convs(dve):
            win_stats_1(dve, cA, 0, 0, 1, 2)
            dve.wait_ge(s_wrest, 16 * 3)
            win_stats_2(dve, cA, 0)
            win_stats_3(dve, cA, 0)
            win_weights(dve, cA, 0)
            for g in range(NG):
                low_parts(dve, cA, 0, g)
            win_stats_1(dve, cA1, 1, 0, 1, 2)
            win_stats_2(dve, cA1, 1)
            win_stats_3(dve, cA1, 1)
            win_weights(dve, cA1, 1)
            for g in range(NG):
                low_parts(dve, cA1, 1, g)

        @block.vector
        def _(dve):
            for c in (cA, cA1, cD):
                dve.memset(c.win[:, 0, :], 0.0)
                dve.memset(c.win[:, NBLK - 1, :], 0.0).then_inc(s_zero, 1)
            dve.wait_ge(s_cst, 16)
            dve.wait_ge(s_wld, 16)
            for dy in range(TAPS):
                stationary(dve, cA, dy)
            first_convs(dve)
            dve.wait_ge(s_x1, x1_moved(1))
            dve.wait_ge(s_x1_pool, 16 * n_x1_pool)
            row_stats_1(dve, x1, sB_bn, 0)
            row_stats_1(dve, x1, sB_bn, 1)
            link = Chain(dve, s_chainB, perB, 0)
            row_stats_2(dve, link, sB_bn, sB_sum, tB, 0)
            row_stats_3(dve, link, sB_sum, sB_ve, tB, 0)
            dve_rows_B_end(dve, link, 0)
            cycles(dve, dve_cycle)
            dve_end(dve)

        @block.tensor
        def _(pe):
            pe.wait_ge(s_cst, 16)
            pe.wait_ge(s_init, 3 + 2 * 2)
            win_mean(pe, cA, 0)
            win_var(pe, cA, 0)
            for g in range(NG):
                conv_group(pe, cA, 0, g, None)
                if g == 2:
                    win_mean(pe, cA1, 1)
                if g == 3:
                    win_var(pe, cA1, 1)
            for g in range(NG):
                conv_group(pe, cA1, 1, g, (cA, 0))
                if g == 3:
                    row_mean(pe, sB_bn, sB_sum, 0)
            row_var(pe, sB_bn, sB_sum, 0)
            cycles(pe, pe_cycle)
            pe_end(pe)


def kernel(x, L0_conv_weights, L0_conv_biases, L2_conv_weight, L3_conv_K):
    import concourse.bacc as bacc
    from concourse.bass_utils import run_bass_kernel_spmd

    def taps(w):
        return np.ascontiguousarray(w)

    arrays = {
        "x": np.ascontiguousarray(x),
        "w0": taps(np.transpose(np.asarray(L0_conv_weights), (1, 2, 3, 0))),
        "b0": np.ascontiguousarray(L0_conv_biases),
        "w2": taps(np.transpose(np.asarray(L2_conv_weight)[:, :, ::-1, ::-1], (1, 2, 3, 0))),
        "w3": taps(np.asarray(L3_conv_K).reshape(C, TAPS, TAPS, C)),
        "consts": shape_constants(),
    }
    nc = bacc.Bacc("TRN2", target_bir_lowering=False, num_devices=1)
    args = [nc.dram_tensor(n, a.shape, mybir.dt.from_np(a.dtype), kind="ExternalInput").ap()
            for n, a in arrays.items()]
    y = nc.dram_tensor("y", (B, C, H, W), mybir.dt.float32, kind="ExternalOutput").ap()
    rows_dram = nc.dram_tensor("rows_dram", (H + 2, C, W), mybir.dt.float32, kind="Internal").ap()
    build(nc, *args, y, rows_dram)
    r = run_bass_kernel_spmd(nc, [arrays], core_ids=[0])
    return r.results[0]["y"]
```
